# Optimizing a Trainium2 kernel written in Bass

```python
import numpy as np
import jax
import jax.numpy as jnp

def _softmax(x, axis=-1):
    return jax.nn.softmax(x, axis=axis)

def _gelu(x):
    return jax.nn.gelu(x, approximate=True)

def _silu(x):
    return jax.nn.silu(x)

def _sigmoid(x):
    return jax.nn.sigmoid(x)

def _layernorm(x, axis=-1, eps=1e-05):
    m = jnp.mean(x, axis=axis, keepdims=True)
    v = jnp.var(x, axis=axis, keepdims=True)
    return (x - m) / jnp.sqrt(v + eps)

def _scatter_add(tgt, idx, src, axis=0):
    return tgt.at[idx].add(src)

def _segment_sum(src, seg, n):
    return jax.ops.segment_sum(src, seg, n)
kernel_name = 'mk_seq_postln_d1_jaxref_r8_04103b'

def setup_inputs(seed: int=0):
    np.random.seed(seed)
    _w = jnp.asarray

    def _L0_attn_setup():
        import jax, jax.numpy as jnp
        import numpy as np
        B_SZ, T, D_IN, H = (8, 128, 128, 128)
        key = jax.random.key(seed)
        ks = jax.random.split(key, 9)
        lim_u = 1.0 / np.sqrt(D_IN)
        return {'x': jax.random.normal(ks[0], (B_SZ, T, D_IN), dtype=jnp.float32), 'W_u': jax.random.uniform(ks[1], (H, D_IN), jnp.float32, -lim_u, lim_u), 'b_u': jax.random.uniform(ks[2], (H,), jnp.float32, -lim_u, lim_u), 'W_g': jax.random.uniform(ks[3], (H, D_IN), jnp.float32, -lim_u, lim_u), 'b_g': jax.random.uniform(ks[4], (H,), jnp.float32, -lim_u, lim_u), 'A': jnp.eye(H, dtype=jnp.float32) * 0.6, 'Bm': jax.random.normal(ks[5], (H, H), dtype=jnp.float32), 'Cm': jax.random.normal(ks[6], (H, H), dtype=jnp.float32), 'D': jax.random.normal(ks[7], (H,), dtype=jnp.float32)}
    _L0_attn_in = _L0_attn_setup()

    def _L0_ffn_setup():
        import jax, jax.numpy as jnp
        import numpy as np
        E, K, D = (8, 2, 128)
        B, S = (2, 512)

        def _layernorm(x, g, b, eps=1e-06):
            m = jnp.mean(x, axis=-1, keepdims=True)
            v = jnp.var(x, axis=-1, keepdims=True)
            return (x - m) * jax.lax.rsqrt(v + eps) * g + b
        key = jax.random.key(seed)
        ks = jax.random.split(key, 6)
        n = lambda k, shape, scale: jax.random.normal(k, shape, jnp.float32) * scale
        return {'x': n(ks[0], (B, S, D), 1.0), 'gate_w': n(ks[1], (D, E), 0.02), 'w1': n(ks[2], (E, D, 2 * D), 0.02), 'b1': jnp.zeros((E, 2 * D), jnp.float32), 'w2': n(ks[3], (E, 2 * D, D), 0.02), 'b2': jnp.zeros((E, D), jnp.float32), 'ln_g': jnp.ones((E, D), jnp.float32), 'ln_b': jnp.zeros((E, D), jnp.float32)}
    _L0_ffn_in = _L0_ffn_setup()
    _d = {'L0_attn_x': _L0_attn_in['x'], 'L0_attn_W_u': _L0_attn_in['W_u'], 'L0_attn_b_u': _L0_attn_in['b_u'], 'L0_attn_W_g': _L0_attn_in['W_g'], 'L0_attn_b_g': _L0_attn_in['b_g'], 'L0_attn_A': _L0_attn_in['A'], 'L0_attn_Bm': _L0_attn_in['Bm'], 'L0_attn_Cm': _L0_attn_in['Cm'], 'L0_attn_D': _L0_attn_in['D'], 'L0_ffn_gate_w': _L0_ffn_in['gate_w'], 'L0_ffn_w1': _L0_ffn_in['w1'], 'L0_ffn_b1': _L0_ffn_in['b1'], 'L0_ffn_w2': _L0_ffn_in['w2'], 'L0_ffn_b2': _L0_ffn_in['b2'], 'L0_ffn_ln_g': _L0_ffn_in['ln_g'], 'L0_ffn_ln_b': _L0_ffn_in['ln_b']}
    _x0 = _d['L0_attn_x']
    _d['L0_attn_x'] = jax.random.normal(jax.random.fold_in(jax.random.key(seed), 1), (4, 1024, 128), dtype=_x0.dtype)
    del _x0
    return _d

def reference(L0_attn_x, L0_attn_W_u, L0_attn_b_u, L0_attn_W_g, L0_attn_b_g, L0_attn_A, L0_attn_Bm, L0_attn_Cm, L0_attn_D, L0_ffn_gate_w, L0_ffn_w1, L0_ffn_b1, L0_ffn_w2, L0_ffn_b2, L0_ffn_ln_g, L0_ffn_ln_b):

    def _L0_attn_ref(x, W_u, b_u, W_g, b_g, A, Bm, Cm, D):
        import jax, jax.numpy as jnp
        import numpy as np
        B_SZ, T, D_IN, H = (8, 128, 128, 128)
        u = jax.nn.gelu(jnp.einsum('btd,hd->bth', x, W_u) + b_u, approximate=False) * jax.nn.sigmoid(jnp.einsum('btd,hd->bth', x, W_g) + b_g)
        uB = jnp.einsum('btd,hd->tbh', u, Bm)

        def step(s, uB_t):
            s = s @ A.T + uB_t
            y = s @ Cm.T + D
            return (s, y)
        s0 = jnp.zeros((x.shape[0], A.shape[0]), dtype=x.dtype)
        _, ys = jax.lax.scan(step, s0, uB)
        return jnp.transpose(ys, (1, 0, 2))

    def _L0_ffn_ref(x, gate_w, w1, b1, w2, b2, ln_g, ln_b):
        import jax, jax.numpy as jnp
        import numpy as np
        E, K, D = (8, 2, 128)
        B, S = (2, 512)

        def _layernorm(x, g, b, eps=1e-06):
            m = jnp.mean(x, axis=-1, keepdims=True)
            v = jnp.var(x, axis=-1, keepdims=True)
            return (x - m) * jax.lax.rsqrt(v + eps) * g + b
        orig_shape = x.shape
        xt = x.reshape(-1, orig_shape[-1])
        scores = xt @ gate_w
        ew, ei = jax.lax.top_k(scores, K)
        ew = jax.nn.softmax(ew, axis=-1)
        mask = ei[None, :, :] == jnp.arange(E)[:, None, None]
        wE = jnp.sum(ew[None, :, :] * mask, axis=-1)
        h = jax.nn.gelu(jnp.einsum('td,edf->etf', xt, w1) + b1[:, None, :], approximate=False)
        o = jnp.einsum('etf,efd->etd', h, w2) + b2[:, None, :]
        y = _layernorm(xt[None, :, :] + o, ln_g[:, None, :], ln_b[:, None, :])
        out = jnp.einsum('et,etd->td', wE, y)
        return out.reshape(orig_shape)
    x = L0_attn_x
    x = _layernorm(x + _L0_attn_ref(x, L0_attn_W_u, L0_attn_b_u, L0_attn_W_g, L0_attn_b_g, L0_attn_A, L0_attn_Bm, L0_attn_Cm, L0_attn_D), axis=-1)
    x = _layernorm(x + _L0_ffn_ref(x, L0_ffn_gate_w, L0_ffn_w1, L0_ffn_b1, L0_ffn_w2, L0_ffn_b2, L0_ffn_ln_g, L0_ffn_ln_b), axis=-1)
    return x

_drawn_inputs = setup_inputs


def setup_inputs(seed=0):
    import zlib

    import numpy as np

    out = dict(_drawn_inputs(seed))
    spreads = {'L0_ffn_b1': (0.0, 0.8),
     'L0_ffn_b2': (0.0, 0.292),
     'L0_ffn_ln_g': (1.0, 0.2),
     'L0_ffn_ln_b': (0.0, 0.1)}
    factors = {'L0_ffn_w1': 4.121, 'L0_ffn_w2': 3.805}
    for name, (base, spread) in spreads.items():
        noise = np.random.default_rng([zlib.crc32(name.encode()), seed]).standard_normal(out[name].shape)
        drawn = base * np.exp(spread * noise) if base else spread * noise
        out[name] = jnp.asarray(drawn.astype(out[name].dtype))
    for name, factor in factors.items():
        out[name] = (out[name] * factor).astype(out[name].dtype)
    return out
```

```python
from contextlib import ExitStack

import concourse.bass as bass
from concourse import mybir

F32 = mybir.dt.float32
BF16 = mybir.dt.bfloat16
I32 = mybir.dt.int32
ALU = mybir.AluOpType
ACT = mybir.ActivationFunctionType
AX = mybir.AxisListType

P = 128
RSQRT_MAGIC = 0x5F3759DF
R_CHAIN = [(0, None, 0, 1), (0, 0, 1, 1), (1, 0, 2, 2), (2, 0, 4, 4), (3, 0, 8, 4), (3, 4, 12, 4)]
CARRY_STEPS = 6
NORM_STEPS = 17
FIRST_STEPS = 4 + NORM_STEPS + 1 + 4 + 2
ROUTE_STEPS = 26
TILE_STEPS = 3
OUT_STEPS = 3 + 4 + NORM_STEPS + 1
TABLE_STEPS = 12
SCALE_STEPS = 13


class Turn:

    def __init__(self, engine, name, first, step, reached):
        self.engine, self.step, self.reached = engine, step, reached
        self.value = engine.alloc_register(name)
        engine.reg_mov(self.value, first)

    def next(self):
        self.engine.reg_add(self.value, self.value, self.step)

    def wait(self, *sems):
        self.engine.wait_ge(self.reached, 1)
        for s in sems:
            self.engine.wait_ge(s, self.value)


class Steps:

    def __init__(self, engine, sem, per_group):
        self.engine, self.sem, self.per_group = engine, sem, per_group
        self.g, self.k = 0, 0

    def open(self, g):
        self.g, self.k = g, 0

    def step(self, instruction):
        instruction.then_inc(self.sem, 1)
        self.k += 1

    def value(self):
        return self.g * self.per_group + self.k

    def wait(self):
        self.engine.wait_ge(self.sem, self.value())

    def link(self, instruction):
        self.step(instruction)
        self.wait()

    def close(self):
        assert self.k == self.per_group, self.k


def later(k, n):
    return not isinstance(k, int) or k >= n


def mixer_moe_kernel(nc, x, W_u, b_u, W_g, b_g, A, Bm, Cm, D, gate_w, w1, b1, w2, b2, ln_g, ln_b, out):
    NSEQ, T, DIM = x.shape
    E = gate_w.shape[1]
    HID = w1.shape[2]
    FC = HID // P
    L = 16
    CH = T // L
    HALF = NSEQ * T // (P * L)
    COLS = HALF * P
    SPG = 2
    TPG = SPG * HALF
    GW = TPG * P
    GROUPS = L // SPG
    ROWS = 2 + E * FC
    SQUARINGS = 9
    TOP = 2
    TOKENS = NSEQ * T
    EPS1 = 1e-5
    EPS_MOE = 1e-6
    PAYS = 3
    CAP = TOKENS + P
    PAD_TILE = E * CAP
    XW = DIM + 1
    YW = DIM + 2
    NX = 8
    NY = 4
    TILES = TOP * TOKENS // P + E
    AHEAD = 2
    assert DIM == P and HALF == 2 and GW == 512 and CH * 2 == P and E == 8 and FC == 2
    assert TILES % NX == 0 and TILES >= TOP * TOKENS // P + E - 1

    xv = x.rearrange("b t d -> (b t) d").rearrange("(h p l) d -> p h l d", h=HALF, p=P)
    ov = out.rearrange("b t d -> (b t) d").rearrange("(h p l) d -> p h l d", h=HALF, p=P)
    buckets = nc.dram_tensor("buckets", (E * CAP + P, XW), F32, kind="Internal").ap()
    y_rows = nc.dram_tensor("y_rows", (TOKENS * TOP, YW), F32, kind="Internal").ap()
    yv = y_rows.rearrange("(h p l k) c -> p h l k c", h=HALF, p=P, k=TOP)

    with ExitStack() as ctx:
        def sb(name, shape, dt=F32):
            return ctx.enter_context(nc.sbuf_tensor(name, shape, dt))

        def sem(name):
            return ctx.enter_context(nc.semaphore(name))

        bank = [ctx.enter_context(nc.psum_tensor(f"bank{i}", [P, 512], F32)) for i in range(8)]
        ps_u, ps_gt, ps_setup, ps_small = bank[0], bank[1], bank[2], bank[3]
        ps_state, ps_pow, ps_xt = [bank[4], bank[5]], bank[6], bank[7]
        ps_carry = bank[2]
        ps_y, ps_score, ps_w = bank[6], bank[0], bank[1]
        ps_tx, ps_hid, ps_o = [bank[4], bank[5]], [bank[6], bank[7]], [bank[2], bank[3]]
        RANK0 = TPG * E
        COUNT0 = 2 * TPG * E

        ident = sb("ident", [P, P])
        before = sb("before", [P, P], BF16)
        ones = sb("ones", [P, P], BF16)
        rev = sb("rev", [P, TPG, E])
        bucket0 = sb("bucket0", [P, TPG, E])
        ids = sb("ids", [P, TOP, GROUPS, TPG], I32)
        tile_no_i = sb("tile_no_i", [1, TILES + AHEAD], I32)
        tile_no = sb("tile_no", [1, TILES + AHEAD])
        pad = sb("pad", [P, XW])
        wraw = sb("wraw", [P, 4, P])
        rows = sb("rows", [ROWS, P])
        bcol = sb("bcol", [P, ROWS])
        half_bg = sb("half_bg", [P, 1])
        wT = sb("wT", [P, 4, P])
        power = [sb(f"power{i}", [P, 2, P]) for i in range(2)]
        pq = sb("pq", [P, SQUARINGS + 1, 2, P])
        R = sb("R", [P, L, P])
        dbc = sb("dbc", [P, P])
        gate_sb = sb("gate_sb", [P, E])
        w1_sb = sb("w1_sb", [P, E * HID])
        w2_sb = sb("w2_sb", [P, E * FC * P])
        b2bc = sb("b2bc", [P, E * P])
        gbc = sb("gbc", [P, E * P])
        lnb_sb = sb("lnb_sb", [E, P])
        x_all = sb("x_all", [P, HALF, L, P])
        xin = [sb(f"xin{i}", [P, HALF, SPG, P]) for i in range(2)]
        xT = [sb(f"xT{i}", [P, GW]) for i in range(2)]
        gelu_u = sb("gelu_u", [P, GW])
        tanh_g = sb("tanh_g", [P, GW])
        u = [sb(f"u{i}", [P, GW]) for i in range(2)]
        local = sb("local", [P, (L + 1) * COLS])
        ends = sb("ends", [P, NSEQ, CH + 1])
        carry = sb("carry", [P, COLS])
        sloc = sb("sloc", [P, SPG, HALF, P])
        z1 = sb("z1", [P, TPG, P])
        st1 = sb("st1", [P, TPG, 6])
        tmp1 = sb("tmp1", [P, 6, TPG])
        rstd1 = sb("rstd1", [P, TPG])
        nb1 = sb("nb1", [P, TPG])
        pay = [[sb(f"pay{k}_{i}", [P, TPG, XW]) for i in range(PAYS)] for k in range(TOP)]
        dest = [sb(f"dest{i}", [P, TOP, TPG], I32) for i in range(PAYS)]
        x1T = sb("x1T", [P, GW])
        m12 = sb("m12", [P, 6, TPG])
        sel = sb("sel", [P, 9, TPG, E])
        chosen = sb("chosen", [P, TPG, E], BF16)
        seen = sb("seen", [P, TPG + 1, E], BF16)
        weight = sb("weight", [P, TOP, GROUPS * TPG])
        wE = sb("wE", [P, TPG, E])
        wET = sb("wET", [E, GW])
        x1b = sb("x1b", [P, GROUPS * TPG, P])
        cnt = sb("cnt", [1, 4, E])
        cnt_i = sb("cnt_i", [1, E], I32)
        passed = sb("passed", [1, TILES + AHEAD, E])
        tabf = sb("tabf", [1, 2, TILES + AHEAD])
        tile_row = sb("tile_row", [1, TILES + AHEAD], I32)
        tile_expert = sb("tile_expert", [1, TILES + AHEAD], I32)
        pad_row = sb("pad_row", [1, E], I32)
        xb = [sb(f"xb{i}", [P, XW]) for i in range(NX)]
        w1_now = [sb(f"w1_now{i}", [P, HID]) for i in range(2)]
        xbT = [sb(f"xbT{i}", [P, P]) for i in range(2)]
        hidden = [sb(f"hidden{i}", [P, FC, P]) for i in range(2)]
        zt = [sb(f"zt{i}", [P, P]) for i in range(2)]
        stz = [sb(f"stz{i}", [P, 6]) for i in range(2)]
        yb = [sb(f"yb{i}", [P, YW]) for i in range(NY)]
        yin = sb("yin", [P, GROUPS * TPG * TOP, YW])
        var = sb("var", [P, 16])
        tmp2 = sb("tmp2", [P, 6, 16])
        scale = [sb(f"scale{i}", [P, TPG, TOP]) for i in range(2)]
        t0 = [sb(f"t0_{i}", [P, TPG, P]) for i in range(2)]
        acc0 = [sb(f"acc0_{i}", [P, TPG, P]) for i in range(2)]
        acc = [sb(f"acc{i}", [P, TPG, P]) for i in range(2)]
        st2 = sb("st2", [P, TPG, 6])
        rstd2 = [sb(f"rstd2_{i}", [P, TPG]) for i in range(2)]
        nb2 = [sb(f"nb2_{i}", [P, TPG]) for i in range(2)]
        obuf = [sb(f"obuf{i}", [P, TPG, P]) for i in range(2)]

        mixer_weights_in = sem("mixer_weights_in")
        moe_weights_in = sem("moe_weights_in")
        x_all_in = sem("x_all_in")
        x_in = [sem(f"x_in{i}") for i in range(2)]
        ident_zeroed = sem("ident_zeroed")
        ident_ready = sem("ident_ready")
        zeros_ready = sem("zeros_ready")
        route_consts_ready = sem("route_consts_ready")
        setup_transposed = sem("setup_transposed")
        setup_copied = sem("setup_copied")
        squared = sem("squared")
        power_ready = sem("power_ready")
        r_product = sem("r_product")
        r_ready = sem("r_ready")
        x_transposed = sem("x_transposed")
        xT_ready = sem("xT_ready")
        u_product = sem("u_product")
        activated = sem("activated")
        u_ready = sem("u_ready")
        state_product = sem("state_product")
        state_ready = sem("state_ready")
        ends_ready = sem("ends_ready")
        carry_product = sem("carry_product")
        carry_ready = sem("carry_ready")
        xd_ready = sem("xd_ready")
        sloc_ready = sem("sloc_ready")
        y_product = sem("y_product")
        z1_ready = sem("z1_ready")
        first_steps = sem("first_steps")
        route_steps = sem("route_steps")
        norm1_ready = sem("norm1_ready")
        x1_ready = sem("x1_ready")
        x1_transposed = sem("x1_transposed")
        x1T_ready = sem("x1T_ready")
        scores_ready = sem("scores_ready")
        gap_ready = sem("gap_ready")
        seen_ready = sem("seen_ready")
        ranks_ready = sem("ranks_ready")
        dest_ready = sem("dest_ready")
        tanh_ready = sem("tanh_ready")
        wE_ready = sem("wE_ready")
        wE_transposed = sem("wE_transposed")
        wET_ready = sem("wET_ready")
        bias_product = sem("bias_product")
        x1b_ready = sem("x1b_ready")
        scattered = [sem(f"scattered{i}") for i in range(PAYS)]
        counts_ready = sem("counts_ready")
        table_steps = sem("table_steps")
        table_ready = sem("table_ready")
        pads_in = sem("pads_in")
        xb_in = [sem(f"xb_in{i}") for i in range(NX)]
        w1_copied = sem("w1_copied")
        xb_transposed = sem("xb_transposed")
        xbT_ready = sem("xbT_ready")
        up_product = sem("up_product")
        hidden_ready = sem("hidden_ready")
        down_product = sem("down_product")
        z_ready = sem("z_ready")
        tile_steps = sem("tile_steps")
        yb_ready = sem("yb_ready")
        yb_stored = [sem(f"yb_stored{i}") for i in range(NY)]
        yin_in = [sem(f"yin_in{i}") for i in range(2)]
        scale_steps = sem("scale_steps")
        out_steps = sem("out_steps")
        scale_ready = sem("scale_ready")
        t0_ready = sem("t0_ready")
        acc0_ready = sem("acc0_ready")
        acc_ready = sem("acc_ready")
        norm2_ready = sem("norm2_ready")
        out_ready = sem("out_ready")
        out_stored = [sem(f"out_stored{i}") for i in range(2)]

        block = ctx.enter_context(nc.Block())

        MIXER_LOADS = 9
        MOE_LOADS = 6
        SETUP_COPIES = 6
        CARRIES = CARRY_STEPS

        def block_of(l):
            return bass.ds(l * COLS, COLS)

        def expert(engine, k):
            return engine.value_load(tile_expert[0:1, bass.ds(k, 1)], min_val=0, max_val=E - 1)

        def scatters_done(engine):
            for i in range(PAYS):
                engine.wait_ge(scattered[i], 16 * TOP * TPG * len(range(i, GROUPS, PAYS)))

        @block.sync
        def _(sp):
            def load_group(g, half, par, reused):
                if reused:
                    sp.wait_ge(x_transposed, g - 1)
                sp.dma_start(xin[par][:], xv[:, :, bass.ds(g * SPG, SPG), :]).then_inc(x_in[par], 16)

            for k, w in enumerate((W_u, W_g, Bm, Cm)):
                sp.dma_start(wraw[:, k, :], w).then_inc(mixer_weights_in, 16)
            sp.dma_start(pq[:, 0, 0, :], A).then_inc(mixer_weights_in, 16)
            sp.dma_start(rows[0:1, :], b_u.rearrange("(a n) -> a n", a=1)).then_inc(mixer_weights_in, 16)
            sp.dma_start(rows[1:2, :], b_g.rearrange("(a n) -> a n", a=1)).then_inc(mixer_weights_in, 16)
            sp.dma_start(rows[2:ROWS, :], b1.rearrange("e (f p) -> (e f) p", p=P)).then_inc(mixer_weights_in, 16)
            sp.dma_start(dbc[:], D.partition_broadcast(P)).then_inc(mixer_weights_in, 16)
            load_group(0, 0, 0, False)
            load_group(1, 0, 1, False)
            sp.dma_start(x_all[:], xv).then_inc(x_all_in, 16)
            with sp.Fori(1, GROUPS // 2) as i:
                load_group(2 * i, i, 0, True)
                load_group(2 * i + 1, i, 1, True)
            sp.dma_start(gate_sb[:], gate_w).then_inc(moe_weights_in, 16)
            sp.dma_start(lnb_sb[:], ln_b).then_inc(moe_weights_in, 16)
            sp.dma_start(w1_sb[:].rearrange("p (e f) -> p e f", e=E), w1.rearrange("e d f -> d e f"))\
                .then_inc(moe_weights_in, 16)
            sp.dma_start(w2_sb[:].rearrange("p (e c d) -> p e c d", e=E, c=FC),
                         w2.rearrange("e (c f) d -> f e c d", c=FC)).then_inc(moe_weights_in, 16)
            sp.dma_start(b2bc[:], b2.rearrange("e d -> (e d)").partition_broadcast(P)).then_inc(moe_weights_in, 16)
            sp.dma_start(gbc[:], ln_g.rearrange("e d -> (e d)").partition_broadcast(P)).then_inc(moe_weights_in, 16)

            sp.wait_ge(route_consts_ready, 7)
            sp.dma_start(buckets[PAD_TILE:PAD_TILE + P, :], pad[:]).then_inc(pads_in, 16)
            sp.wait_ge(table_ready, 1)
            for e in range(E):
                r = sp.value_load(pad_row[0:1, e:e + 1], min_val=e * CAP, max_val=e * CAP + TOKENS)
                sp.dma_start(buckets[bass.ds(r, P), :], pad[:]).then_inc(pads_in, 16)
            sp.wait_ge(pads_in, 16 * (E + 1))
            scatters_done(sp)

            def load_tile(k, slot, turn):
                if turn is not None:
                    sp.wait_ge(yb_stored[slot % NY], 16 * turn)
                r = sp.value_load(tile_row[0:1, bass.ds(k, 1)], min_val=0, max_val=PAD_TILE)
                sp.dma_start(xb[slot][:], buckets[bass.ds(r, P), :]).then_inc(xb_in[slot], 16)

            for k in range(NX):
                load_tile(k, k, None)
            with sp.Fori(1, TILES // NX) as i:
                for s in range(NX):
                    load_tile(i * NX + s, s, (NX // NY) * (i - 1) + s // NY + 1)
            for s in range(AHEAD):
                load_tile(TILES + s, s, (NX // NY) * (TILES // NX - 1) + s // NY + 1)

            for i in range(NY):
                sp.wait_ge(yb_stored[i], 16 * (TILES // NY))

            def load_y(g, par, turn):
                if turn is not None:
                    sp.wait_ge(yin_in[par], 16 * turn)
                c = TPG * TOP
                sp.dma_start(yin[:, bass.ds(g * c, c), :].rearrange("p (h l k) c -> p h l k c", h=HALF, k=TOP),
                             yv[:, :, bass.ds(g * SPG, SPG), :, :]).then_inc(yin_in[par], 16)

            load_y(0, 0, None)
            load_y(1, 1, None)
            with sp.Fori(1, GROUPS // 2) as i:
                load_y(2 * i, 0, i)
                load_y(2 * i + 1, 1, i)

            def store(g, par):
                sp.wait_ge(out_ready, g + 1)
                sp.dma_start(ov[:, :, bass.ds(g * SPG, SPG), :],
                             obuf[par][:].rearrange("p (h l) d -> p h l d", h=HALF)).then_inc(out_stored[par], 16)

            with sp.Fori(0, GROUPS // 2) as i:
                store(2 * i, 0)
                store(2 * i + 1, 1)
            for par in range(2):
                sp.wait_ge(out_stored[par], 16 * (GROUPS // 2))
            for s in range(AHEAD):
                sp.wait_ge(xb_in[s], 16 * (TILES // NX + 1))

        @block.tensor
        def _(pe):
            mm, tr = nc.tensor.matmul, nc.tensor.transpose

            pe.wait_ge(mixer_weights_in, 16 * MIXER_LOADS)
            pe.wait_ge(ident_ready, 1)
            for k in range(4):
                tr(ps_setup[:, k * P:(k + 1) * P], wraw[:, k, :], ident[:])
            tr(ps_small[:, 0:P], pq[:, 0, 0, :], ident[:])
            mm(ps_small[:, P:P + ROWS], rows[:], ident[0:ROWS, 0:ROWS], start=True, stop=True)\
                .then_inc(setup_transposed, 1)
            pe.wait_ge(setup_copied, SETUP_COPIES)

            def transpose_x(g, half, par, first=False):
                pe.wait_ge(x_in[par], 16 * (half + 1))
                if not first:
                    pe.wait_ge(xT_ready, g)
                for l in range(SPG):
                    for h in range(HALF):
                        c = (l * HALF + h) * P
                        ins = tr(ps_xt[:, c:c + P], xin[par][:, h, l, :], ident[:])
                ins.then_inc(x_transposed, 1)

            def gates(g, par, first=False):
                pe.wait_ge(xT_ready, g + 1)
                if not first:
                    pe.wait_ge(activated, 2 * g)
                mm(ps_u[:], wT[:, 0, :], xT[par][:], start=True, stop=True).then_inc(u_product, 1)
                mm(ps_gt[:], wT[:, 1, :], xT[par][:], start=True, stop=True).then_inc(u_product, 1)

            def state_step(g, l, par, first=False):
                s = g * SPG + l
                pe.wait_ge(u_ready, g + 1)
                if not first:
                    pe.wait_ge(state_ready, s - 1)
                mm(ps_state[l][:, 0:COLS], wT[:, 2, :], u[par][:, l * COLS:(l + 1) * COLS], start=True, stop=False)
                pe.wait_ge(state_ready, s)
                mm(ps_state[l][:, 0:COLS], pq[:, 0, 1, :], local[:, block_of(s)], start=False, stop=True)\
                    .then_inc(state_product, 1)

            def square(k, a, at):
                if k is not None:
                    pe.wait_ge(power_ready, k)
                mm(ps_pow[:, 0:P], at, a, start=True, stop=True)
                mm(ps_pow[:, P:2 * P], a, at, start=True, stop=True).then_inc(squared, 1)

            def mixer_group(g, half, par, first=False):
                state_step(g, 0, par, first)
                square(g + 1, power[1 - par][:, 0, :], power[1 - par][:, 1, :])
                transpose_x(g + 1, half + par, 1 - par)
                state_step(g, 1, par, first)
                gates(g + 1, 1 - par)

            transpose_x(0, 0, 0, True)
            gates(0, 0, True)
            square(None, pq[:, 0, 0, :], pq[:, 0, 1, :])
            pe.wait_ge(zeros_ready, 1)
            mixer_group(0, 0, 0, True)
            with pe.Fori(0, GROUPS // 2 - 1) as i:
                mixer_group(2 * i + 1, i, 1)
                mixer_group(2 * i + 2, i + 1, 0)
            state_step(GROUPS - 1, 0, 1)
            square(GROUPS, power[0][:, 0, :], power[0][:, 1, :])
            state_step(GROUPS - 1, 1, 1)

            pe.wait_ge(power_ready, SQUARINGS)
            for n, (k, src, dst, width) in enumerate(R_CHAIN):
                pe.wait_ge(r_ready, n)
                rhs = wT[:, 3, :] if src is None else R[:, src:src + width, :].rearrange("p l d -> p (l d)")
                mm(ps_small[:, 0:width * P], pq[:, k, 0, :], rhs, start=True, stop=True).then_inc(r_product, 1)
                d = 1 << n
                pe.wait_ge(ends_ready, n + 1)
                mm(ps_carry[:, 0:NSEQ * (CH - d)].rearrange("p (b c) -> p b c", b=NSEQ),
                   pq[:, 4 + n, 1, :], ends[:, :, 1:CH + 1 - d], start=True, stop=True).then_inc(carry_product, 1)

            def mixer_out(g):
                pe.wait_ge(sloc_ready, g + 1)
                if later(g, 1):
                    pe.wait_ge(z1_ready, g)
                for h in range(HALF):
                    for l in range(SPG):
                        c = (h * SPG + l) * P
                        mm(ps_y[:, c:c + P], sloc[:, l, h, :], wT[:, 3, :], start=True, stop=False)
                        ins = mm(ps_y[:, c:c + P], carry[:, h * P:(h + 1) * P],
                                 R[:, bass.ds(g * SPG + l, 1), :].rearrange("p l d -> p (l d)"),
                                 start=False, stop=True)
                ins.then_inc(y_product, 1)

            def transpose_x1(g, b):
                pe.wait_ge(x1_ready, g + 1)
                if later(g, 1):
                    pe.wait_ge(x1T_ready, g)
                for j in range(TPG):
                    ins = tr(ps_xt[:, j * P:(j + 1) * P], pay[0][b][:, j, 0:P], ident[:])
                ins.then_inc(x1_transposed, 1)

            def scores(g):
                pe.wait_ge(x1T_ready, g + 1)
                for j in range(TPG):
                    ins = mm(ps_score[:, j * E:(j + 1) * E], x1T[:, j * P:(j + 1) * P], gate_sb[:],
                             start=True, stop=True)
                ins.then_inc(scores_ready, 1)

            def ranks(g):
                pe.wait_ge(seen_ready, g + 1)
                o = ps_score[:, RANK0:RANK0 + TPG * E]
                mm(o, before[:], chosen[:].rearrange("p j e -> p (j e)"), start=True, stop=False)
                mm(o, ones[:], seen[:, 0:TPG, :].rearrange("p j e -> p (j e)"), start=False, stop=True)\
                    .then_inc(ranks_ready, 1)

            def transpose_weights(g):
                pe.wait_ge(wE_ready, g + 1)
                if later(g, 1):
                    pe.wait_ge(x1b_ready, g)
                for j in range(TPG):
                    ins = mm(ps_w[0:E, j * P:(j + 1) * P], wE[:, j, :], ident[:], start=True, stop=True)
                ins.then_inc(wE_transposed, 1)

            def bias(g):
                pe.wait_ge(wET_ready, g + 1)
                for j in range(TPG):
                    ins = mm(ps_w[:, j * P:(j + 1) * P], wET[:, j * P:(j + 1) * P], lnb_sb[:], start=True, stop=True)
                ins.then_inc(bias_product, 1)

            def route_group(g, b, last=False):
                if not last:
                    mixer_out(g + 1)
                scores(g)
                ranks(g)
                if not last:
                    transpose_x1(g + 1, (b + 1) % PAYS)
                transpose_weights(g)
                bias(g)

            pe.wait_ge(carry_ready, 1)
            pe.wait_ge(r_ready, len(R_CHAIN))
            pe.wait_ge(route_consts_ready, 7)
            pe.wait_ge(moe_weights_in, 16 * MOE_LOADS)
            mixer_out(0)
            transpose_x1(0, 0)
            route_group(0, 0)
            with pe.Fori(0, (GROUPS - 2) // PAYS) as i:
                for c in range(PAYS):
                    route_group(i * PAYS + 1 + c, (1 + c) % PAYS)
            route_group(GROUPS - 1, (GROUPS - 1) % PAYS, last=True)
            mm(ps_score[:, COUNT0:COUNT0 + E], ones[:], seen[:, TPG, :], start=True, stop=True)\
                .then_inc(counts_ready, 1)

            def transpose_tile(k, slot, turn):
                pe.wait_ge(xb_in[slot], 16 * (turn + 1))
                if later(k, 2):
                    pe.wait_ge(xbT_ready, k - 1)
                tr(ps_tx[slot % 2][:, 0:P], xb[slot][:, 0:P], ident[:]).then_inc(xb_transposed, 1)

            def up(k, slot):
                pe.wait_ge(xbT_ready, k + 1)
                pe.wait_ge(w1_copied, k + 1)
                if later(k, 2):
                    pe.wait_ge(hidden_ready, k - 1)
                for c in range(FC):
                    ins = mm(ps_hid[slot % 2][:, c * P:(c + 1) * P], w1_now[slot % 2][:, c * P:(c + 1) * P],
                             xbT[slot % 2][:], start=True, stop=True)
                ins.then_inc(up_product, 1)

            def down(k, slot):
                e = expert(pe, k)
                pe.wait_ge(hidden_ready, k + 1)
                if later(k, 2):
                    pe.wait_ge(z_ready, k - 1)
                for c in range(FC):
                    ins = mm(ps_o[slot % 2][:, 0:P], hidden[slot % 2][:, c, :],
                             w2_sb[:, bass.ds(e * (FC * P) + c * P, P)], start=(c == 0), stop=(c == FC - 1))
                ins.then_inc(down_product, 1)

            def expert_tiles(i):
                for s in range(NX):
                    k = i * NX + s
                    transpose_tile(k + AHEAD, (s + AHEAD) % NX, i + (s + AHEAD) // NX)
                    up(k + 1, (s + 1) % NX)
                    down(k, s)

            pe.wait_ge(table_ready, 1)
            for k in range(AHEAD):
                transpose_tile(k, k, 0)
            up(0, 0)
            expert_tiles(0)
            with pe.Fori(1, TILES // NX) as i:
                expert_tiles(i)

        @block.scalar
        def _(act):
            f = nc.scalar.activation

            def gate_activations(g, first=False):
                act.wait_ge(u_product, 2 * g + 1)
                if not first:
                    act.wait_ge(u_ready, g)
                f(gelu_u[:], ps_u[:], ACT.Gelu, bias=bcol[:, 0:1]).then_inc(activated, 1)
                act.wait_ge(u_product, 2 * g + 2)
                f(tanh_g[:], ps_gt[:], ACT.Tanh, bias=half_bg[:], scale=0.5).then_inc(activated, 1)

            act.wait_ge(setup_copied, SETUP_COPIES)
            gate_activations(0, True)
            with act.Fori(1, GROUPS) as g:
                gate_activations(g)

            def stage_states(g):
                if later(g, 1):
                    act.wait_ge(y_product, g)
                f(sloc[:].rearrange("p l h c -> p (l h c)"),
                  local[:, bass.ds((g * SPG + 1) * COLS, GW)], ACT.Copy).then_inc(sloc_ready, 1)

            def normalise_x1(g, b, turn):
                act.wait_ge(norm1_ready, g + 1)
                act.wait_ge(scattered[b], 16 * TOP * TPG * turn)
                if later(g, 2):
                    act.wait_ge(x1b_ready, g - 2)
                for j in range(TPG):
                    ins = f(pay[0][b][:, j, 0:P], z1[:, j, :], ACT.Identity, bias=nb1[:, j:j + 1],
                            scale=rstd1[:, j:j + 1])
                ins.then_inc(x1_ready, 1)

            def copy_x1T(g):
                act.wait_ge(x1_transposed, g + 1)
                if later(g, 1):
                    act.wait_ge(scores_ready, g)
                f(x1T[:], ps_xt[:], ACT.Copy).then_inc(x1T_ready, 1)

            def gap_tanh(g):
                act.wait_ge(gap_ready, g + 1)
                f(m12[:, 5, :], m12[:, 4, :], ACT.Tanh, scale=0.5).then_inc(tanh_ready, 1)

            def copy_weights(g):
                act.wait_ge(wE_transposed, g + 1)
                if later(g, 1):
                    act.wait_ge(bias_product, g)
                f(wET[:], ps_w[0:E, :], ACT.Copy).then_inc(wET_ready, 1)

            def route_group(g, b, turn, last=False):
                if not last:
                    stage_states(g + 1)
                gap_tanh(g)
                if not last:
                    normalise_x1(g + 1, (b + 1) % PAYS, turn)
                    copy_x1T(g + 1)
                copy_weights(g)

            act.wait_ge(state_ready, L)
            stage_states(0)
            normalise_x1(0, 0, 0)
            copy_x1T(0)
            route_group(0, 0, 0)
            with act.Fori(0, (GROUPS - 2) // PAYS) as i:
                for c in range(PAYS):
                    route_group(i * PAYS + 1 + c, (1 + c) % PAYS, i + (2 + c) // PAYS)
            route_group(GROUPS - 1, (GROUPS - 1) % PAYS, None, last=True)

            def copy_xbT(k, slot):
                act.wait_ge(xb_transposed, k + 1)
                if later(k, 2):
                    act.wait_ge(up_product, k - 1)
                f(xbT[slot % 2][:], ps_tx[slot % 2][:, 0:P], ACT.Copy).then_inc(xbT_ready, 1)

            def gelu(k, slot):
                e = expert(act, k)
                act.wait_ge(up_product, k + 1)
                if later(k, 2):
                    act.wait_ge(down_product, k - 1)
                for c in range(FC):
                    ins = f(hidden[slot % 2][:, c, :], ps_hid[slot % 2][:, c * P:(c + 1) * P], ACT.Gelu,
                            bias=bcol[:, bass.ds(e * FC + 2 + c, 1)])
                ins.then_inc(hidden_ready, 1)

            def expert_tiles(i):
                for s in range(NX):
                    k = i * NX + s
                    copy_xbT(k + AHEAD, (s + AHEAD) % NX)
                    gelu(k + 1, (s + 1) % NX)

            act.wait_ge(table_ready, 1)
            for k in range(AHEAD):
                copy_xbT(k, k)
            gelu(0, 0)
            expert_tiles(0)
            with act.Fori(1, TILES // NX) as i:
                expert_tiles(i)

            def weigh_first(g, par):
                act.wait_ge(scale_ready, g + 1)
                if later(g, 2):
                    act.wait_ge(acc0_ready, g - 1)
                for j in range(TPG):
                    ins = f(t0[par][:, j, :],
                            yin[:, bass.ds((g * TPG + j) * TOP, 1), 0:P].rearrange("p a d -> p (a d)"),
                            ACT.Copy, scale=scale[par][:, j, 0:1])
                ins.then_inc(t0_ready, 1)

            def normalise_out(g, par, turn):
                act.wait_ge(norm2_ready, g + 1)
                if turn is not None:
                    act.wait_ge(out_stored[par], 16 * turn)
                for j in range(TPG):
                    ins = f(obuf[par][:, j, :], acc[par][:, j, :], ACT.Identity, bias=nb2[par][:, j:j + 1],
                            scale=rstd2[par][:, j:j + 1])
                ins.then_inc(out_ready, 1)

            weigh_first(0, 0)
            weigh_first(1, 1)
            for g in range(2):
                normalise_out(g, g, None)
                weigh_first(g + 2, g)
            with act.Fori(1, GROUPS // 2 - 1) as i:
                for par in range(2):
                    normalise_out(2 * i + par, par, i)
                    weigh_first(2 * i + par + 2, par)
            for par in range(2):
                normalise_out(GROUPS - 2 + par, par, GROUPS // 2 - 1)

        @block.vector
        def _(dve):
            v = nc.vector
            cp, tt, ts, stt = v.tensor_copy, v.tensor_tensor, v.tensor_scalar, v.scalar_tensor_tensor

            def halves_sum_and_variance(steps, st, tmp, q, n, eps):
                me, mo, qe, qo = st[:, 0:n, 1], st[:, 0:n, 4], st[:, 0:n, 2], st[:, 0:n, 5]
                d, s, dd = (tmp[:, i, 0:n] for i in range(3))
                steps.step(tt(d, me, mo, ALU.subtract))
                steps.step(tt(s, me, mo, ALU.add))
                steps.link(tt(q, qe, qo, ALU.add))
                steps.step(stt(dd, d, 0.25, d, ALU.mult, ALU.mult))
                steps.link(ts(q, q, 1.0 / P, eps, ALU.mult, ALU.add))
                steps.link(tt(q, q, dd, ALU.add))
                return s

            def rsqrt(steps, q, tmp, n):
                a, y = tmp[:, 4, 0:n], tmp[:, 5, 0:n]
                yi = y.bitcast(I32)
                steps.link(ts(yi, q.bitcast(I32), 1, None, ALU.logical_shift_right))
                steps.link(ts(yi, yi, -1.0, float(RSQRT_MAGIC), ALU.mult, ALU.add))
                for _ in range(3):
                    steps.link(tt(a, y, y, ALU.mult))
                    steps.link(stt(a, a, -0.5, q, ALU.mult, ALU.mult))
                    steps.link(stt(y, a, 1.5, y, ALU.add, ALU.mult))
                return y

            dve.wait_ge(setup_transposed, 1)
            cp(wT[:, 0:2, :].rearrange("p k d -> p (k d)"), ps_setup[:, 0:2 * P]).then_inc(setup_copied, 1)
            ts(wT[:, 2, :], ps_setup[:, 2 * P:3 * P], 0.5, None, ALU.mult).then_inc(setup_copied, 1)
            cp(wT[:, 3, :], ps_setup[:, 3 * P:4 * P]).then_inc(setup_copied, 1)
            cp(pq[:, 0, 1, :], ps_small[:, 0:P]).then_inc(setup_copied, 1)
            cp(bcol[:], ps_small[:, P:P + ROWS]).then_inc(setup_copied, 1)
            ts(half_bg[:], ps_small[:, P + 1:P + 2], 0.5, None, ALU.mult).then_inc(setup_copied, 1)

            def copy_xT(g, par, first=False):
                dve.wait_ge(x_transposed, g + 1)
                if not first:
                    dve.wait_ge(u_product, 2 * (g - 1))
                cp(xT[par][:], ps_xt[:]).then_inc(xT_ready, 1)

            def make_u(g, par, first=False):
                dve.wait_ge(activated, 2 * g + 2)
                if not first:
                    dve.wait_ge(state_product, SPG * (g - 1))
                stt(u[par][:], tanh_g[:], 1.0, gelu_u[:], ALU.add, ALU.mult).then_inc(u_ready, 1)

            def copy_state(g, l):
                s = g * SPG + l
                dve.wait_ge(state_product, s + 1)
                cp(local[:, block_of(s + 1)], ps_state[l][:, 0:COLS]).then_inc(state_ready, 1)

            def copy_power(k, par):
                dve.wait_ge(squared, k)
                cp(power[par][:].rearrange("p a d -> p (a d)"), ps_pow[:, 0:2 * P])
                cp(pq[:, bass.ds(k, 1), :, :].rearrange("p k a d -> p (k a d)"), ps_pow[:, 0:2 * P])\
                    .then_inc(power_ready, 1)

            def mixer_group(g, par, first=False):
                copy_state(g, 0)
                copy_power(g + 2, par)
                copy_xT(g + 1, 1 - par, first)
                copy_state(g, 1)
                make_u(g + 1, 1 - par, first)

            copy_xT(0, 0, True)
            copy_power(1, 1)
            make_u(0, 0, True)
            mixer_group(0, 0, True)
            with dve.Fori(0, GROUPS // 2 - 1) as i:
                mixer_group(2 * i + 1, 1)
                mixer_group(2 * i + 2, 0)
            copy_state(GROUPS - 1, 0)
            copy_power(SQUARINGS, 1)
            copy_state(GROUPS - 1, 1)

            dve.wait_ge(zeros_ready, 2)
            dve.wait_ge(state_ready, L)
            cp(ends[:, :, 1:CH + 1], local[:, L * COLS:(L + 1) * COLS].rearrange("p (b c) -> p b c", b=NSEQ))\
                .then_inc(ends_ready, 1)
            for n, (k, src, dst, width) in enumerate(R_CHAIN):
                dve.wait_ge(r_product, n + 1)
                cp(R[:, dst:dst + width, :].rearrange("p l d -> p (l d)"), ps_small[:, 0:width * P]).then_inc(r_ready, 1)
                d = 1 << n
                dve.wait_ge(carry_product, n + 1)
                dve.wait_ge(ends_ready, n + 1)
                tt(ends[:, :, 1 + d:CH + 1], ends[:, :, 1 + d:CH + 1],
                   ps_carry[:, 0:NSEQ * (CH - d)].rearrange("p (b c) -> p b c", b=NSEQ), ALU.add).then_inc(ends_ready, 1)
            dve.wait_ge(ends_ready, CARRY_STEPS + 1)
            cp(carry[:].rearrange("p (b c) -> p b c", b=NSEQ), ends[:, :, 0:CH]).then_inc(carry_ready, 1)

            first = Steps(dve, first_steps, FIRST_STEPS)
            route = Steps(dve, route_steps, ROUTE_STEPS)

            def first_norm(g):
                dve.wait_ge(y_product, g + 1)
                dve.wait_ge(xd_ready, 1)
                if later(g, 1):
                    dve.wait_ge(x1_ready, g)
                    dve.wait_ge(first_steps, g * FIRST_STEPS)
                first.open(g)
                tt(z1[:].rearrange("p (h l) d -> p h l d", h=HALF),
                   ps_y[:].rearrange("p (h l d) -> p h l d", h=HALF, l=SPG),
                   x_all[:, :, bass.ds(g * SPG, SPG), :], ALU.add).then_inc(z1_ready, 1)
                dve.wait_ge(z1_ready, g + 1)
                for j in range(TPG):
                    first.step(v.bn_stats(st1[:, j, :], z1[:, j, :]))
                first.wait()

            def first_norm_scales(g):
                s = halves_sum_and_variance(first, st1, tmp1, tmp1[:, 3, :], TPG, EPS1)
                y = rsqrt(first, tmp1[:, 3, :], tmp1, TPG)
                first.step(cp(rstd1[:], y))
                stt(nb1[:], s, -0.5, y, ALU.mult, ALU.mult).then_inc(norm1_ready, 1)
                dve.wait_ge(norm1_ready, g + 1)

            def second_payload(g, b, turn):
                dve.wait_ge(scattered[b], 16 * TOP * TPG * turn)
                for j in range(TPG):
                    first.step(ts(pay[1][b][:, j, 0:P], z1[:, j, :], rstd1[:, j:j + 1], nb1[:, j:j + 1],
                                  ALU.mult, ALU.add))
                for k in range(TOP):
                    first.step(cp(pay[k][b][:, :, P:XW].bitcast(I32).rearrange("p j a -> p (j a)"),
                                  ids[:, k, bass.ds(g, 1), :].rearrange("p g j -> p (g j)")))
                first.close()

            eq1, oh1, s2, eq2, oh2, both, diff, place, part = (sel[:, i] for i in range(9))
            m1, r1, m2, r2, gap, th = (m12[:, i, :] for i in range(6))

            def spread(a):
                return a.unsqueeze(2).broadcast_to([P, TPG, E])

            def top2(g):
                dve.wait_ge(scores_ready, g + 1)
                route.wait()
                sc = ps_score[:, 0:TPG * E].rearrange("p (j e) -> p j e", e=E)
                route.link(v.tensor_reduce(m1, sc, AX.X, ALU.max))
                route.link(tt(eq1, sc, spread(m1), ALU.is_equal))
                route.link(tt(eq1, eq1, rev[:], ALU.mult))
                route.link(v.tensor_reduce(r1, eq1, AX.X, ALU.max))
                route.link(tt(oh1, eq1, spread(r1), ALU.is_equal))
                route.link(stt(s2, oh1, -3.0e38, sc, ALU.mult, ALU.add))
                route.link(v.tensor_reduce(m2, s2, AX.X, ALU.max))
                tt(gap, m2, m1, ALU.subtract).then_inc(gap_ready, 1)
                route.link(tt(eq2, s2, spread(m2), ALU.is_equal))
                route.link(tt(eq2, eq2, rev[:], ALU.mult))
                route.link(v.tensor_reduce(r2, eq2, AX.X, ALU.max))
                route.link(tt(oh2, eq2, spread(r2), ALU.is_equal))
                route.link(tt(both, oh1, oh2, ALU.add))
                route.step(tt(diff, oh2, oh1, ALU.subtract))
                if later(g, 1):
                    dve.wait_ge(ranks_ready, g)
                route.step(cp(chosen[:], both))
                route.link(cp(seen[:, 0, :], seen[:, TPG, :]))
                for j in range(TPG):
                    ins = tt(seen[:, j + 1, :], seen[:, j, :], both[:, j, :], ALU.add)
                    if j < TPG - 1:
                        route.link(ins)
                    else:
                        ins.then_inc(seen_ready, 1)

            def destinations(g, b):
                dve.wait_ge(ranks_ready, g + 1)
                rk = ps_score[:, RANK0:RANK0 + TPG * E].rearrange("p (j e) -> p j e", e=E)
                route.link(tt(place, rk, bucket0[:], ALU.add))
                for k, oh in enumerate((oh1, oh2)):
                    route.link(tt(part, oh, place, ALU.mult))
                    with nc.allow_low_precision(reason="row numbers, exact in float32, to int32"):
                        ins = v.tensor_reduce(dest[b][:, k, :], part, AX.X, ALU.add)
                    if k == 0:
                        route.link(ins)
                    else:
                        ins.then_inc(dest_ready, 1)

            def weights(g):
                dve.wait_ge(tanh_ready, g + 1)
                if later(g, 1):
                    dve.wait_ge(wE_transposed, g)
                for k in range(TOP):
                    route.step(ts(weight[:, k, bass.ds(g * TPG, TPG)], th, (-0.5, 0.5)[k], 0.5, ALU.mult, ALU.add))
                route.link(tt(diff, diff, spread(th), ALU.mult))
                route.link(tt(both, both, diff, ALU.add))
                ts(wE[:], both, 0.5, None, ALU.mult).then_inc(wE_ready, 1)
                route.close()

            def add_bias(g, b):
                dve.wait_ge(bias_product, g + 1)
                dve.wait_ge(x1_ready, g + 1)
                tt(x1b[:, bass.ds(g * TPG, TPG), :], ps_w[:].rearrange("p (j d) -> p j d", d=P),
                   pay[0][b][:, :, 0:P], ALU.add).then_inc(x1b_ready, 1)

            def route_group(g, b, turn, last=False):
                route.open(g)
                top2(g)
                if not last:
                    first_norm(g + 1)
                destinations(g, b)
                if not last:
                    first_norm_scales(g + 1)
                    second_payload(g + 1, (b + 1) % PAYS, turn)
                weights(g)
                add_bias(g, b)

            first_norm(0)
            first_norm_scales(0)
            second_payload(0, 0, 0)
            route_group(0, 0, 0)
            with dve.Fori(0, (GROUPS - 2) // PAYS) as i:
                for c in range(PAYS):
                    route_group(i * PAYS + 1 + c, (1 + c) % PAYS, i + (2 + c) // PAYS)
            route_group(GROUPS - 1, (GROUPS - 1) % PAYS, None, last=True)

            table = Steps(dve, table_steps, TABLE_STEPS)
            tokens, tiles, upto, skip = (cnt[:, i, :] for i in range(4))
            every = [1, TILES + AHEAD, E]
            dve.wait_ge(counts_ready, 1)
            table.step(cp(tile_no[:], tile_no_i[:]))
            table.link(cp(tokens, ps_score[0:1, COUNT0:COUNT0 + E]))
            table.link(ts(cnt_i[:], tokens, float(P - 1), None, ALU.add))
            table.link(ts(cnt_i[:], cnt_i[:], 7, None, ALU.logical_shift_right))
            table.link(cp(tiles, cnt_i[:]))
            table.link(v.tensor_tensor_scan(upto, skip, tiles, 0.0, ALU.mult, ALU.add))
            table.step(ts(skip, tiles, -float(P), float(CAP), ALU.mult, ALU.add))
            table.link(tt(passed[:], tile_no[:].unsqueeze(2).broadcast_to(every), upto.unsqueeze(1).broadcast_to(every),
                          ALU.is_ge))
            table.link(v.tensor_reduce(tabf[:, 0, :], passed[:], AX.X, ALU.add))
            table.link(tt(passed[:], passed[:], skip.unsqueeze(1).broadcast_to(every), ALU.mult))
            table.link(v.tensor_reduce(tabf[:, 1, :], passed[:], AX.X, ALU.add))
            ts(tile_expert[:], tabf[:, 0, :], float(E - 1), None, ALU.min)
            tt(pad_row[:], tokens, bucket0[0:1, 0, :], ALU.add)
            table.link(stt(tabf[:, 1, :], tile_no[:], float(P), tabf[:, 1, :], ALU.mult, ALU.add))
            ts(tile_row[:], tabf[:, 1, :], float(PAD_TILE), None, ALU.min).then_inc(table_ready, 1)
            table.close()
            dve.wait_ge(table_ready, 1)

            tile = Steps(dve, tile_steps, TILE_STEPS)
            statistics = Turn(dve, "statistics", 2, TILE_STEPS, table_ready)

            def copy_w1(k, slot):
                e = expert(dve, k)
                if later(k, 2):
                    dve.wait_ge(up_product, k - 1)
                cp(w1_now[slot % 2][:], w1_sb[:, bass.ds(e * HID, HID)]).then_inc(w1_copied, 1)
                return e

            def tile_rows(k, slot, e, turn):
                tile.open(k)
                buf, y = zt[slot % 2], yb[slot % NY]
                dve.wait_ge(down_product, k + 1)
                tt(buf[:], ps_o[slot % 2][:, 0:P], xb[slot][:, 0:P], ALU.add).then_inc(z_ready, 1)
                dve.wait_ge(z_ready, k + 1)
                tile.link(tt(buf[:], buf[:], b2bc[:, bass.ds(e * P, P)], ALU.add))
                if later(k, NY):
                    dve.wait_ge(yb_stored[slot % NY], 16 * turn)
                tile.step(v.bn_stats(stz[slot % 2][:], buf[:]))
                statistics.wait(tile_steps)
                statistics.next()
                tile.link(v.bn_aggr(y[:, P:YW], stz[slot % 2][:]))
                stt(y[:, 0:P], buf[:], y[:, P:P + 1], gbc[:, bass.ds(e * P, P)], ALU.subtract, ALU.mult)\
                    .then_inc(yb_ready, 1)
                tile.close()

            def expert_tiles(i, es):
                for s in range(NX):
                    k = i * NX + s
                    es.append(copy_w1(k + AHEAD, (s + AHEAD) % NX))
                    tile_rows(k, s, es.pop(0), (NX // NY) * i + s // NY)

            expert_tiles(0, [copy_w1(k, k) for k in range(AHEAD)])
            with dve.Fori(1, TILES // NX) as i:
                expert_tiles(i, [expert(dve, i * NX + s) for s in range(AHEAD)])

            early = Steps(dve, scale_steps, SCALE_STEPS)
            late = Steps(dve, out_steps, OUT_STEPS)
            GC = TPG * TOP

            def load_variances(g, q):
                return ts(q, yin[:, bass.ds(g * GC, GC), P + 1:P + 2].rearrange("p a b -> p (a b)"),
                          EPS_MOE, None, ALU.add)

            def scales(g, par, y):
                tt(scale[par][:], y.rearrange("p (j k) -> p j k", k=TOP),
                   weight[:, :, bass.ds(g * TPG, TPG)].rearrange("p k j -> p j k"), ALU.mult).then_inc(scale_ready, 1)

            for g in range(2):
                dve.wait_ge(yin_in[g], 16)
                early.step(load_variances(g, var[:, g * GC:(g + 1) * GC]))
            early.wait()
            y = rsqrt(early, var[:], tmp2, 2 * GC)
            early.close()
            for g in range(2):
                scales(g, g, y[:, g * GC:(g + 1) * GC])

            def output_group(g, par, half, last=False):
                late.open(g)
                dve.wait_ge(acc0_ready, g + 1)
                if later(g, 2):
                    dve.wait_ge(out_ready, g - 1)
                dve.wait_ge(scale_ready, g + 1)
                for j in range(TPG):
                    ins = stt(acc[par][:, j, :],
                              yin[:, bass.ds((g * TPG + j) * TOP + 1, 1), 0:P].rearrange("p a d -> p (a d)"),
                              scale[par][:, j, 1:2], acc0[par][:, j, :], ALU.mult, ALU.add)
                    if j < TPG - 1:
                        late.step(ins)
                    else:
                        ins.then_inc(acc_ready, 1)
                dve.wait_ge(acc_ready, g + 1)
                for j in range(TPG):
                    late.step(v.bn_stats(st2[:, j, :], acc[par][:, j, :]))
                if not last:
                    dve.wait_ge(yin_in[par], 16 * (half + 2))
                    load_variances(g + 2, var[:, TPG:TPG + GC])
                late.wait()
                s = halves_sum_and_variance(late, st2, tmp2, var[:, 0:TPG], TPG, EPS1)
                n = TPG if last else TPG + GC
                y = rsqrt(late, var[:, 0:n], tmp2, n)
                late.step(cp(rstd2[par][:], y[:, 0:TPG]))
                stt(nb2[par][:], s, -0.5, y[:, 0:TPG], ALU.mult, ALU.mult).then_inc(norm2_ready, 1)
                if not last:
                    dve.wait_ge(t0_ready, g + 1)
                    scales(g + 2, par, y[:, TPG:n])
                late.close()

            output_group(0, 0, 0)
            output_group(1, 1, 0)
            with dve.Fori(1, GROUPS // 2 - 1) as i:
                output_group(2 * i, 0, i)
                output_group(2 * i + 1, 1, i)
            output_group(GROUPS - 2, 0, None, last=True)
            output_group(GROUPS - 1, 1, None, last=True)

        @block.gpsimd
        def _(pool):
            gp = nc.gpsimd
            gp.memset(ident[:], 0.0).then_inc(ident_zeroed, 1)
            pool.wait_ge(ident_zeroed, 1)
            gp.affine_select(out=ident[:], in_=ident[:], compare_op=ALU.not_equal, fill=1.0, base=0,
                             pattern=[[-1, P]], channel_multiplier=1).then_inc(ident_ready, 1)
            gp.memset(local[:, 0:COLS], 0.0).then_inc(zeros_ready, 1)
            gp.memset(ends[:], 0.0).then_inc(zeros_ready, 1)
            pool.wait_ge(x_all_in, 16)
            pool.wait_ge(mixer_weights_in, 16 * MIXER_LOADS)
            gp.tensor_tensor(x_all[:].rearrange("p h l d -> p (h l) d"), x_all[:].rearrange("p h l d -> p (h l) d"),
                             dbc[:].unsqueeze(1).broadcast_to([P, HALF * L, P]), ALU.add).then_inc(xd_ready, 1)
            gp.memset(before[:], 1.0).then_inc(route_consts_ready, 1)
            gp.memset(pad[:], 0.0).then_inc(route_consts_ready, 1)
            for e in range(E):
                gp.memset(rev[:, :, e], float(E - e))
                gp.memset(bucket0[:, :, e], float(e * CAP))
            gp.memset(ones[:], 1.0)
            gp.memset(seen[:], 0.0)
            gp.memset(cnt[:, 3, :], 1.0).then_inc(route_consts_ready, 1)
            gp.iota(tile_no_i[:], pattern=[[1, TILES + AHEAD]], base=0, channel_multiplier=0)\
                .then_inc(route_consts_ready, 1)
            gp.iota(ids[:].rearrange("p k g (h l) -> p k g h l", h=HALF),
                    pattern=[[1, TOP], [SPG * TOP, GROUPS], [P * L * TOP, HALF], [TOP, SPG]], base=0,
                    channel_multiplier=L * TOP).then_inc(route_consts_ready, 1)
            pool.wait_ge(route_consts_ready, 5)
            gp.affine_select(out=before[:], in_=before[:], compare_op=ALU.is_gt, fill=0.0, base=0,
                             pattern=[[1, P]], channel_multiplier=-1).then_inc(route_consts_ready, 1)
            gp.memset(pad[:, P:XW].bitcast(I32), TOKENS * TOP).then_inc(route_consts_ready, 1)

            def scatter_group(g, b):
                routed.wait(x1_ready, dest_ready)
                for k in range(TOP):
                    for j in range(TPG):
                        pool.indirect_dma_start(
                            buckets, bass.IndirectOffsetOnAxis(ap=dest[b][:, k, j:j + 1], axis=0),
                            pay[k][b][:, j, :], None).then_inc(scattered[b], 16)
                routed.next()

            routed = Turn(pool, "routed", 1, 1, xd_ready)
            scatter_group(0, 0)
            with pool.Fori(0, (GROUPS - 2) // PAYS) as i:
                for c in range(PAYS):
                    scatter_group(i * PAYS + 1 + c, (1 + c) % PAYS)
            scatter_group(GROUPS - 1, (GROUPS - 1) % PAYS)

            def scatter_tile(k, slot):
                made.wait(yb_ready)
                pool.indirect_dma_start(
                    y_rows, bass.IndirectOffsetOnAxis(ap=xb[slot][:, P:XW].bitcast(I32), axis=0), yb[slot % NY][:],
                    None, bounds_check=TOKENS * TOP - 1, oob_is_err=False).then_inc(yb_stored[slot % NY], 16)
                made.next()

            made = Turn(pool, "made", 1, 1, table_ready)
            with pool.Fori(0, TILES // NX) as i:
                for s in range(NX):
                    scatter_tile(i * NX + s, s)

            def add_x1(g, par):
                pool.wait_ge(t0_ready, g + 1)
                if later(g, 2):
                    pool.wait_ge(acc_ready, g - 1)
                gp.tensor_tensor(acc0[par][:], t0[par][:], x1b[:, bass.ds(g * TPG, TPG), :], ALU.add)\
                    .then_inc(acc0_ready, 1)

            pool.wait_ge(x1b_ready, GROUPS)
            add_x1(0, 0)
            add_x1(1, 1)
            with pool.Fori(1, GROUPS // 2) as i:
                add_x1(2 * i, 0)
                add_x1(2 * i + 1, 1)


_INS = ['L0_attn_x', 'L0_attn_W_u', 'L0_attn_b_u', 'L0_attn_W_g', 'L0_attn_b_g', 'L0_attn_A', 'L0_attn_Bm',
        'L0_attn_Cm', 'L0_attn_D', 'L0_ffn_gate_w', 'L0_ffn_w1', 'L0_ffn_b1', 'L0_ffn_w2', 'L0_ffn_b2',
        'L0_ffn_ln_g', 'L0_ffn_ln_b']
_OUTS = [((4, 1024, 128), 'float32')]


def kernel(**inputs):
    import numpy as _np
    import concourse.bacc as _bacc
    from concourse import mybir as _mybir
    from concourse.bass_utils import run_bass_kernel_spmd as _run

    nc = _bacc.Bacc("TRN2", target_bir_lowering=False, num_devices=1)
    arrays, args = {}, []
    for name in _INS:
        a = _np.ascontiguousarray(inputs[name])
        arrays[f"in_{name}_dram"] = a
        args.append(nc.dram_tensor(f"in_{name}_dram", a.shape, _mybir.dt.from_np(a.dtype), kind="ExternalInput").ap())
    for i, (shape, dtype) in enumerate(_OUTS):
        dt = _mybir.dt.from_np(_np.dtype(dtype))
        args.append(nc.dram_tensor(f"out_{i}_dram", shape, dt, kind="ExternalOutput").ap())
    mixer_moe_kernel(nc, *args)
    r = _run(nc, [arrays], core_ids=[0])
    got = tuple(r.results[0][f"out_{i}_dram"] for i in range(len(_OUTS)))
    return got[0]
```

```python
from contextlib import ExitStack

import concourse.bass as bass
from concourse import mybir

F32 = mybir.dt.float32
BF16 = mybir.dt.bfloat16
I32 = mybir.dt.int32
ALU = mybir.AluOpType
ACT = mybir.ActivationFunctionType
AX = mybir.AxisListType

P = 128
RSQRT_MAGIC = 0x5F3759DF
R_CHAIN = [(0, None, 0, 1), (0, 0, 1, 1), (1, 0, 2, 2), (2, 0, 4, 4), (3, 0, 8, 4), (3, 4, 12, 4)]
CARRY_STEPS = 6
NORM_STEPS = 17
FIRST_STEPS = 4 + NORM_STEPS + 1 + 4 + 2
ROUTE_STEPS = 26
TILE_STEPS = 12
OUT_STEPS = 3 + 4 + NORM_STEPS + 1
TABLE_STEPS = 12
SCALE_STEPS = 13


class Turn:

    def __init__(self, engine, name, first, step, reached):
        self.engine, self.step, self.reached = engine, step, reached
        self.value = engine.alloc_register(name)
        engine.reg_mov(self.value, first)

    def next(self):
        self.engine.reg_add(self.value, self.value, self.step)

    def wait(self, *sems):
        self.engine.wait_ge(self.reached, 1)
        for s in sems:
            self.engine.wait_ge(s, self.value)


class Steps:

    def __init__(self, engine, sem, per_group):
        self.engine, self.sem, self.per_group = engine, sem, per_group
        self.g, self.k = 0, 0

    def open(self, g):
        self.g, self.k = g, 0

    def step(self, instruction):
        instruction.then_inc(self.sem, 1)
        self.k += 1

    def value(self):
        return self.g * self.per_group + self.k

    def wait(self):
        self.engine.wait_ge(self.sem, self.value())

    def link(self, instruction):
        self.step(instruction)
        self.wait()

    def close(self):
        assert self.k == self.per_group, self.k


def later(k, n):
    return not isinstance(k, int) or k >= n


def mixer_moe_kernel(nc, x, W_u, b_u, W_g, b_g, A, Bm, Cm, D, gate_w, w1, b1, w2, b2, ln_g, ln_b, out):
    NSEQ, T, DIM = x.shape
    E = gate_w.shape[1]
    HID = w1.shape[2]
    FC = HID // P
    L = 16
    CH = T // L
    HALF = NSEQ * T // (P * L)
    COLS = HALF * P
    SPG = 2
    TPG = SPG * HALF
    GW = TPG * P
    GROUPS = L // SPG
    ROWS = 2 + E * FC
    SQUARINGS = 9
    TOP = 2
    TOKENS = NSEQ * T
    EPS1 = 1e-5
    EPS_MOE = 1e-6
    PAYS = 3
    CAP = TOKENS + P
    PAD_TILE = E * CAP
    XW = DIM + 1
    YW = DIM + 2
    TILES = TOP * TOKENS // P + E
    BT = 4
    NB = 4
    BATCHES = TILES // BT
    LOOPED = BATCHES // NB
    assert DIM == P and HALF == 2 and GW == 512 and CH * 2 == P and E == 8 and FC == 2
    assert TILES % BT == 0 and TILES >= TOP * TOKENS // P + E - 1

    xv = x.rearrange("b t d -> (b t) d").rearrange("(h p l) d -> p h l d", h=HALF, p=P)
    ov = out.rearrange("b t d -> (b t) d").rearrange("(h p l) d -> p h l d", h=HALF, p=P)
    buckets = nc.dram_tensor("buckets", (E * CAP + P, XW), F32, kind="Internal").ap()
    y_rows = nc.dram_tensor("y_rows", (TOKENS * TOP, YW), F32, kind="Internal").ap()
    yv = y_rows.rearrange("(h p l k) c -> p h l k c", h=HALF, p=P, k=TOP)

    with ExitStack() as ctx:
        def sb(name, shape, dt=F32):
            return ctx.enter_context(nc.sbuf_tensor(name, shape, dt))

        def sem(name):
            return ctx.enter_context(nc.semaphore(name))

        bank = [ctx.enter_context(nc.psum_tensor(f"bank{i}", [P, 512], F32)) for i in range(8)]
        ps_u, ps_gt, ps_setup, ps_small = bank[0], bank[1], bank[2], bank[3]
        ps_state, ps_pow, ps_xt = [bank[4], bank[5]], bank[6], bank[7]
        ps_carry = bank[2]
        ps_y, ps_score, ps_w = bank[6], bank[0], bank[1]
        ps_tx, ps_hid, ps_o = [bank[4], bank[5]], [bank[6], bank[7], bank[0], bank[1]], [bank[2], bank[3]]
        RANK0 = TPG * E
        COUNT0 = 2 * TPG * E

        ident = sb("ident", [P, P])
        before = sb("before", [P, P], BF16)
        ones = sb("ones", [P, P], BF16)
        rev = sb("rev", [P, TPG, E])
        bucket0 = sb("bucket0", [P, TPG, E])
        ids = sb("ids", [P, TOP, GROUPS, TPG], I32)
        tile_no_i = sb("tile_no_i", [1, TILES], I32)
        tile_no = sb("tile_no", [1, TILES])
        pad = sb("pad", [P, XW])
        wraw = sb("wraw", [P, 4, P])
        rows = sb("rows", [ROWS, P])
        bcol = sb("bcol", [P, ROWS])
        half_bg = sb("half_bg", [P, 1])
        wT = sb("wT", [P, 4, P])
        power = [sb(f"power{i}", [P, 2, P]) for i in range(2)]
        pq = sb("pq", [P, SQUARINGS + 1, 2, P])
        R = sb("R", [P, L, P])
        dbc = sb("dbc", [P, P])
        gate_sb = sb("gate_sb", [P, E])
        w1_sb = sb("w1_sb", [P, E * HID])
        w2_sb = sb("w2_sb", [P, E * FC * P])
        b2bc = sb("b2bc", [P, E * P])
        gbc = sb("gbc", [P, E * P])
        lnb_sb = sb("lnb_sb", [E, P])
        xin = [sb(f"xin{i}", [P, HALF, SPG, P]) for i in range(2)]
        xT = [sb(f"xT{i}", [P, GW]) for i in range(2)]
        gelu_u = sb("gelu_u", [P, GW])
        tanh_g = sb("tanh_g", [P, GW])
        u = [sb(f"u{i}", [P, GW]) for i in range(2)]
        STATES = (L + 1) * COLS
        YIN = GROUPS * TPG * TOP * YW
        by_token = sb("by_token", [P, max(STATES + HALF * L * P, YIN)])
        local = by_token[:, 0:STATES]
        x_all = by_token[:, STATES:STATES + HALF * L * P].rearrange("p (h l d) -> p h l d", h=HALF, l=L)
        yin = by_token[:, 0:YIN].rearrange("p (a c) -> p a c", c=YW)
        ends = sb("ends", [P, NSEQ, CH + 1])
        carry = sb("carry", [P, COLS])
        sloc = sb("sloc", [P, SPG, HALF, P])
        z1 = sb("z1", [P, TPG, P])
        st1 = sb("st1", [P, TPG, 6])
        tmp1 = sb("tmp1", [P, 6, TPG])
        rstd1 = sb("rstd1", [P, TPG])
        nb1 = sb("nb1", [P, TPG])
        pay = [[sb(f"pay{k}_{i}", [P, TPG, XW]) for i in range(PAYS)] for k in range(TOP)]
        dest = [sb(f"dest{i}", [P, TOP, TPG], I32) for i in range(PAYS)]
        x1T = sb("x1T", [P, GW])
        m12 = sb("m12", [P, 6, TPG])
        sel = sb("sel", [P, 9, TPG, E])
        chosen = sb("chosen", [P, TPG, E], BF16)
        seen = sb("seen", [P, TPG + 1, E], BF16)
        weight = sb("weight", [P, TOP, GROUPS * TPG])
        wE = sb("wE", [P, TPG, E])
        wET = sb("wET", [E, GW])
        x1b = sb("x1b", [P, GROUPS * TPG, P])
        cnt = sb("cnt", [1, 4, E])
        cnt_i = sb("cnt_i", [1, E], I32)
        passed = sb("passed", [1, TILES, E])
        tabf = sb("tabf", [1, 2, TILES])
        tile_row = sb("tile_row", [1, TILES], I32)
        tile_expert = sb("tile_expert", [1, TILES], I32)
        pad_row = sb("pad_row", [1, E], I32)
        xb = [sb(f"xb{i}", [P, BT, XW]) for i in range(NB)]
        w1_now = [sb(f"w1_now{i}", [P, BT, HID]) for i in range(NB)]
        xbT = [sb(f"xbT{i}", [P, BT, P]) for i in range(2)]
        hidden = [sb(f"hidden{i}", [P, BT, FC, P]) for i in range(2)]
        zt = [sb(f"zt{i}", [P, BT, P]) for i in range(2)]
        stz = sb("stz", [P, BT, 6])
        yb = [sb(f"yb{i}", [P, BT, YW]) for i in range(2)]
        row_ids = [sb(f"row_ids{i}", [P, BT], I32) for i in range(NB)]
        var = sb("var", [P, 16])
        tmp2 = sb("tmp2", [P, 6, 16])
        scale = [sb(f"scale{i}", [P, TPG, TOP]) for i in range(2)]
        t0 = [sb(f"t0_{i}", [P, TPG, P]) for i in range(2)]
        acc0 = [sb(f"acc0_{i}", [P, TPG, P]) for i in range(2)]
        acc = [sb(f"acc{i}", [P, TPG, P]) for i in range(2)]
        st2 = sb("st2", [P, TPG, 6])
        rstd2 = [sb(f"rstd2_{i}", [P, TPG]) for i in range(2)]
        nb2 = [sb(f"nb2_{i}", [P, TPG]) for i in range(2)]
        obuf = [sb(f"obuf{i}", [P, TPG, P]) for i in range(2)]

        mixer_weights_in = sem("mixer_weights_in")
        moe_weights_in = sem("moe_weights_in")
        x_all_in = sem("x_all_in")
        x_in = [sem(f"x_in{i}") for i in range(2)]
        ident_zeroed = sem("ident_zeroed")
        ident_ready = sem("ident_ready")
        zeros_ready = sem("zeros_ready")
        route_consts_ready = sem("route_consts_ready")
        setup_transposed = sem("setup_transposed")
        setup_copied = sem("setup_copied")
        squared = sem("squared")
        power_ready = sem("power_ready")
        r_product = sem("r_product")
        r_ready = sem("r_ready")
        x_transposed = sem("x_transposed")
        xT_ready = sem("xT_ready")
        u_product = sem("u_product")
        activated = sem("activated")
        u_ready = sem("u_ready")
        state_product = sem("state_product")
        state_ready = sem("state_ready")
        ends_ready = sem("ends_ready")
        carry_product = sem("carry_product")
        carry_ready = sem("carry_ready")
        xd_ready = sem("xd_ready")
        sloc_ready = sem("sloc_ready")
        y_product = sem("y_product")
        z1_ready = sem("z1_ready")
        first_steps = sem("first_steps")
        route_steps = sem("route_steps")
        norm1_ready = sem("norm1_ready")
        x1_ready = sem("x1_ready")
        x1_transposed = sem("x1_transposed")
        x1T_ready = sem("x1T_ready")
        scores_ready = sem("scores_ready")
        gap_ready = sem("gap_ready")
        seen_ready = sem("seen_ready")
        ranks_ready = sem("ranks_ready")
        dest_ready = sem("dest_ready")
        tanh_ready = sem("tanh_ready")
        wE_ready = sem("wE_ready")
        wE_transposed = sem("wE_transposed")
        wET_ready = sem("wET_ready")
        bias_product = sem("bias_product")
        x1b_ready = sem("x1b_ready")
        scattered = [sem(f"scattered{i}") for i in range(PAYS)]
        counts_ready = sem("counts_ready")
        table_steps = sem("table_steps")
        table_ready = sem("table_ready")
        pads_in = sem("pads_in")
        xb_in = [sem(f"xb_in{i}") for i in range(NB)]
        w1_copied = sem("w1_copied")
        xb_transposed = sem("xb_transposed")
        xbT_ready = sem("xbT_ready")
        up_product = sem("up_product")
        hidden_ready = sem("hidden_ready")
        down_product = sem("down_product")
        z_ready = sem("z_ready")
        ids_kept = sem("ids_kept")
        tile_steps = sem("tile_steps")
        yb_ready = sem("yb_ready")
        yb_stored = [sem(f"yb_stored{i}") for i in range(2)]
        yin_in = [sem(f"yin_in{i}") for i in range(2)]
        scale_steps = sem("scale_steps")
        out_steps = sem("out_steps")
        scale_ready = sem("scale_ready")
        t0_ready = sem("t0_ready")
        acc0_ready = sem("acc0_ready")
        acc_ready = sem("acc_ready")
        norm2_ready = sem("norm2_ready")
        out_ready = sem("out_ready")
        out_stored = [sem(f"out_stored{i}") for i in range(2)]

        block = ctx.enter_context(nc.Block())

        MIXER_LOADS = 9
        MOE_LOADS = 6
        SETUP_COPIES = 6
        CARRIES = CARRY_STEPS

        def block_of(l):
            return bass.ds(l * COLS, COLS)

        def registers(engine, name):
            return [engine.alloc_register(f"{name}{s}") for s in range(BT)]

        def load_batch_of(engine, regs, table, b):
            engine.load(regs, table[0:1, bass.ds(b * BT, BT)])

        def values(engine, regs, top):
            return [engine.snap(r, min_val=0, max_val=top) for r in regs]

        def batches(engine, one):
            for b in range(NB):
                one(b, b, 0)
            with engine.Fori(1, LOOPED) as i:
                for q in range(NB):
                    one(i * NB + q, q, i)
            for b in range(LOOPED * NB, BATCHES):
                one(b, b % NB, b // NB)

        def exists(b):
            return not isinstance(b, int) or b < BATCHES

        def scatters_done(engine):
            for i in range(PAYS):
                engine.wait_ge(scattered[i], 16 * TOP * TPG * len(range(i, GROUPS, PAYS)))

        @block.sync
        def _(sp):
            def load_group(g, half, par, reused):
                if reused:
                    sp.wait_ge(x_transposed, g - 1)
                sp.dma_start(xin[par][:], xv[:, :, bass.ds(g * SPG, SPG), :]).then_inc(x_in[par], 16)

            for k, w in enumerate((W_u, W_g, Bm, Cm)):
                sp.dma_start(wraw[:, k, :], w).then_inc(mixer_weights_in, 16)
            sp.dma_start(pq[:, 0, 0, :], A).then_inc(mixer_weights_in, 16)
            sp.dma_start(rows[0:1, :], b_u.rearrange("(a n) -> a n", a=1)).then_inc(mixer_weights_in, 16)
            sp.dma_start(rows[1:2, :], b_g.rearrange("(a n) -> a n", a=1)).then_inc(mixer_weights_in, 16)
            sp.dma_start(rows[2:ROWS, :], b1.rearrange("e (f p) -> (e f) p", p=P)).then_inc(mixer_weights_in, 16)
            sp.dma_start(dbc[:], D.partition_broadcast(P)).then_inc(mixer_weights_in, 16)
            load_group(0, 0, 0, False)
            load_group(1, 0, 1, False)
            sp.dma_start(x_all, xv).then_inc(x_all_in, 16)
            with sp.Fori(1, GROUPS // 2) as i:
                load_group(2 * i, i, 0, True)
                load_group(2 * i + 1, i, 1, True)
            sp.dma_start(gate_sb[:], gate_w).then_inc(moe_weights_in, 16)
            sp.dma_start(lnb_sb[:], ln_b).then_inc(moe_weights_in, 16)
            sp.dma_start(w1_sb[:].rearrange("p (e f) -> p e f", e=E), w1.rearrange("e d f -> d e f"))\
                .then_inc(moe_weights_in, 16)
            sp.dma_start(w2_sb[:].rearrange("p (e c d) -> p e c d", e=E, c=FC),
                         w2.rearrange("e (c f) d -> f e c d", c=FC)).then_inc(moe_weights_in, 16)
            sp.dma_start(b2bc[:], b2.rearrange("e d -> (e d)").partition_broadcast(P)).then_inc(moe_weights_in, 16)
            sp.dma_start(gbc[:], ln_g.rearrange("e d -> (e d)").partition_broadcast(P)).then_inc(moe_weights_in, 16)

            sp.wait_ge(route_consts_ready, 7)
            sp.dma_start(buckets[PAD_TILE:PAD_TILE + P, :], pad[:]).then_inc(pads_in, 16)
            sp.wait_ge(table_ready, 1)
            for e in range(E):
                r = sp.value_load(pad_row[0:1, e:e + 1], min_val=e * CAP, max_val=e * CAP + TOKENS)
                sp.dma_start(buckets[bass.ds(r, P), :], pad[:]).then_inc(pads_in, 16)
            sp.wait_ge(pads_in, 16 * (E + 1))
            scatters_done(sp)

            def load_batch(b, q, turn):
                if later(b, NB):
                    sp.wait_ge(ids_kept, b - NB + 1)
                load_batch_of(sp, first_rows, tile_row, b)
                for s, r in enumerate(values(sp, first_rows, PAD_TILE)):
                    sp.dma_start(xb[q][:, s, :], buckets[bass.ds(r, P), :]).then_inc(xb_in[q], 16)

            first_rows = registers(sp, "first_row")
            batches(sp, load_batch)

            for i in range(2):
                sp.wait_ge(yb_stored[i], 16 * BT * (BATCHES // 2))

            def load_y(g, par, turn):
                if turn is not None:
                    sp.wait_ge(yin_in[par], 16 * turn)
                c = TPG * TOP
                sp.dma_start(yin[:, bass.ds(g * c, c), :].rearrange("p (h l k) c -> p h l k c", h=HALF, k=TOP),
                             yv[:, :, bass.ds(g * SPG, SPG), :, :]).then_inc(yin_in[par], 16)

            load_y(0, 0, None)
            load_y(1, 1, None)
            with sp.Fori(1, GROUPS // 2) as i:
                load_y(2 * i, 0, i)
                load_y(2 * i + 1, 1, i)

            def store(g, par):
                sp.wait_ge(out_ready, g + 1)
                sp.dma_start(ov[:, :, bass.ds(g * SPG, SPG), :],
                             obuf[par][:].rearrange("p (h l) d -> p h l d", h=HALF)).then_inc(out_stored[par], 16)

            with sp.Fori(0, GROUPS // 2) as i:
                store(2 * i, 0)
                store(2 * i + 1, 1)
            for par in range(2):
                sp.wait_ge(out_stored[par], 16 * (GROUPS // 2))

        @block.tensor
        def _(pe):
            mm, tr = nc.tensor.matmul, nc.tensor.transpose

            pe.wait_ge(mixer_weights_in, 16 * MIXER_LOADS)
            pe.wait_ge(ident_ready, 1)
            for k in range(4):
                tr(ps_setup[:, k * P:(k + 1) * P], wraw[:, k, :], ident[:])
            tr(ps_small[:, 0:P], pq[:, 0, 0, :], ident[:])
            mm(ps_small[:, P:P + ROWS], rows[:], ident[0:ROWS, 0:ROWS], start=True, stop=True)\
                .then_inc(setup_transposed, 1)
            pe.wait_ge(setup_copied, SETUP_COPIES)

            def transpose_x(g, half, par, first=False):
                pe.wait_ge(x_in[par], 16 * (half + 1))
                if not first:
                    pe.wait_ge(xT_ready, g)
                for l in range(SPG):
                    for h in range(HALF):
                        c = (l * HALF + h) * P
                        ins = tr(ps_xt[:, c:c + P], xin[par][:, h, l, :], ident[:])
                ins.then_inc(x_transposed, 1)

            def gates(g, par, first=False):
                pe.wait_ge(xT_ready, g + 1)
                if not first:
                    pe.wait_ge(activated, 2 * g)
                mm(ps_u[:], wT[:, 0, :], xT[par][:], start=True, stop=True).then_inc(u_product, 1)
                mm(ps_gt[:], wT[:, 1, :], xT[par][:], start=True, stop=True).then_inc(u_product, 1)

            def state_step(g, l, par, first=False):
                s = g * SPG + l
                pe.wait_ge(u_ready, g + 1)
                if not first:
                    pe.wait_ge(state_ready, s - 1)
                mm(ps_state[l][:, 0:COLS], wT[:, 2, :], u[par][:, l * COLS:(l + 1) * COLS], start=True, stop=False)
                pe.wait_ge(state_ready, s)
                mm(ps_state[l][:, 0:COLS], pq[:, 0, 1, :], local[:, block_of(s)], start=False, stop=True)\
                    .then_inc(state_product, 1)

            def square(k, a, at):
                if k is not None:
                    pe.wait_ge(power_ready, k)
                mm(ps_pow[:, 0:P], at, a, start=True, stop=True)
                mm(ps_pow[:, P:2 * P], a, at, start=True, stop=True).then_inc(squared, 1)

            def mixer_group(g, half, par, first=False):
                state_step(g, 0, par, first)
                square(g + 1, power[1 - par][:, 0, :], power[1 - par][:, 1, :])
                transpose_x(g + 1, half + par, 1 - par)
                state_step(g, 1, par, first)
                gates(g + 1, 1 - par)

            transpose_x(0, 0, 0, True)
            gates(0, 0, True)
            square(None, pq[:, 0, 0, :], pq[:, 0, 1, :])
            pe.wait_ge(zeros_ready, 1)
            mixer_group(0, 0, 0, True)
            with pe.Fori(0, GROUPS // 2 - 1) as i:
                mixer_group(2 * i + 1, i, 1)
                mixer_group(2 * i + 2, i + 1, 0)
            state_step(GROUPS - 1, 0, 1)
            square(GROUPS, power[0][:, 0, :], power[0][:, 1, :])
            state_step(GROUPS - 1, 1, 1)

            pe.wait_ge(power_ready, SQUARINGS)
            for n, (k, src, dst, width) in enumerate(R_CHAIN):
                pe.wait_ge(r_ready, n)
                rhs = wT[:, 3, :] if src is None else R[:, src:src + width, :].rearrange("p l d -> p (l d)")
                mm(ps_small[:, 0:width * P], pq[:, k, 0, :], rhs, start=True, stop=True).then_inc(r_product, 1)
                d = 1 << n
                pe.wait_ge(ends_ready, n + 1)
                mm(ps_carry[:, 0:NSEQ * (CH - d)].rearrange("p (b c) -> p b c", b=NSEQ),
                   pq[:, 4 + n, 1, :], ends[:, :, 1:CH + 1 - d], start=True, stop=True).then_inc(carry_product, 1)

            def mixer_out(g):
                pe.wait_ge(sloc_ready, g + 1)
                if later(g, 1):
                    pe.wait_ge(z1_ready, g)
                for h in range(HALF):
                    for l in range(SPG):
                        c = (h * SPG + l) * P
                        mm(ps_y[:, c:c + P], sloc[:, l, h, :], wT[:, 3, :], start=True, stop=False)
                        ins = mm(ps_y[:, c:c + P], carry[:, h * P:(h + 1) * P],
                                 R[:, bass.ds(g * SPG + l, 1), :].rearrange("p l d -> p (l d)"),
                                 start=False, stop=True)
                ins.then_inc(y_product, 1)

            def transpose_x1(g, b):
                pe.wait_ge(x1_ready, g + 1)
                if later(g, 1):
                    pe.wait_ge(x1T_ready, g)
                for j in range(TPG):
                    ins = tr(ps_xt[:, j * P:(j + 1) * P], pay[0][b][:, j, 0:P], ident[:])
                ins.then_inc(x1_transposed, 1)

            def scores(g):
                pe.wait_ge(x1T_ready, g + 1)
                for j in range(TPG):
                    ins = mm(ps_score[:, j * E:(j + 1) * E], x1T[:, j * P:(j + 1) * P], gate_sb[:],
                             start=True, stop=True)
                ins.then_inc(scores_ready, 1)

            def ranks(g):
                pe.wait_ge(seen_ready, g + 1)
                o = ps_score[:, RANK0:RANK0 + TPG * E]
                mm(o, before[:], chosen[:].rearrange("p j e -> p (j e)"), start=True, stop=False)
                mm(o, ones[:], seen[:, 0:TPG, :].rearrange("p j e -> p (j e)"), start=False, stop=True)\
                    .then_inc(ranks_ready, 1)

            def transpose_weights(g):
                pe.wait_ge(wE_ready, g + 1)
                if later(g, 1):
                    pe.wait_ge(x1b_ready, g)
                for j in range(TPG):
                    ins = mm(ps_w[0:E, j * P:(j + 1) * P], wE[:, j, :], ident[:], start=True, stop=True)
                ins.then_inc(wE_transposed, 1)

            def bias(g):
                pe.wait_ge(wET_ready, g + 1)
                for j in range(TPG):
                    ins = mm(ps_w[:, j * P:(j + 1) * P], wET[:, j * P:(j + 1) * P], lnb_sb[:], start=True, stop=True)
                ins.then_inc(bias_product, 1)

            def route_group(g, b, last=False):
                if not last:
                    mixer_out(g + 1)
                scores(g)
                ranks(g)
                if not last:
                    transpose_x1(g + 1, (b + 1) % PAYS)
                transpose_weights(g)
                bias(g)

            pe.wait_ge(carry_ready, 1)
            pe.wait_ge(r_ready, len(R_CHAIN))
            pe.wait_ge(route_consts_ready, 7)
            pe.wait_ge(moe_weights_in, 16 * MOE_LOADS)
            mixer_out(0)
            transpose_x1(0, 0)
            route_group(0, 0)
            with pe.Fori(0, (GROUPS - 2) // PAYS) as i:
                for c in range(PAYS):
                    route_group(i * PAYS + 1 + c, (1 + c) % PAYS)
            route_group(GROUPS - 1, (GROUPS - 1) % PAYS, last=True)
            mm(ps_score[:, COUNT0:COUNT0 + E], ones[:], seen[:, TPG, :], start=True, stop=True)\
                .then_inc(counts_ready, 1)

            def transpose_batch(b, q, turn):
                pe.wait_ge(xb_in[q], 16 * BT * (turn + 1))
                if later(b, 2):
                    pe.wait_ge(xbT_ready, b - 1)
                for s in range(BT):
                    ins = tr(ps_tx[q % 2][:, s * P:(s + 1) * P], xb[q][:, s, 0:P], ident[:])
                ins.then_inc(xb_transposed, 1)

            def up(b, q, h):
                if h == 0:
                    pe.wait_ge(xbT_ready, b + 1)
                    pe.wait_ge(w1_copied, b + 1)
                if later(b, 2):
                    pe.wait_ge(hidden_ready, (b - 2) * BT + 2 * h + 2)
                for s in range(2 * h, 2 * h + 2):
                    for c in range(FC):
                        at = (s % 2) * HID + c * P
                        ins = mm(ps_hid[(q % 2) * 2 + h][:, at:at + P], w1_now[q][:, s, c * P:(c + 1) * P],
                                 xbT[q % 2][:, s, :], start=True, stop=True)
                ins.then_inc(up_product, 1)

            def down(b, q, s, e):
                pe.wait_ge(hidden_ready, b * BT + s + 1)
                if s == 0 and later(b, 2):
                    pe.wait_ge(z_ready, b - 1)
                for c in range(FC):
                    ins = mm(ps_o[q % 2][:, s * P:(s + 1) * P], hidden[q % 2][:, s, c, :],
                             w2_sb[:, bass.ds(e * (FC * P) + c * P, P)], start=(c == 0), stop=(c == FC - 1))
                if s == BT - 1:
                    ins.then_inc(down_product, 1)

            def expert_batch(b, q, turn):
                load_batch_of(pe, experts, tile_expert, b)
                e = values(pe, experts, E - 1)
                if exists(b + 2):
                    transpose_batch(b + 2, (q + 2) % NB, turn + (q + 2) // NB)
                for h in range(BT // 2):
                    if exists(b + 1):
                        up(b + 1, (q + 1) % NB, h)
                    for s in range(2 * h, 2 * h + 2):
                        down(b, q, s, e[s])

            experts = registers(pe, "pe_expert")
            pe.wait_ge(table_ready, 1)
            for b in range(2):
                transpose_batch(b, b, 0)
            for h in range(BT // 2):
                up(0, 0, h)
            batches(pe, expert_batch)

        @block.scalar
        def _(act):
            f = nc.scalar.activation

            def gate_activations(g, first=False):
                act.wait_ge(u_product, 2 * g + 1)
                if not first:
                    act.wait_ge(u_ready, g)
                f(gelu_u[:], ps_u[:], ACT.Gelu, bias=bcol[:, 0:1]).then_inc(activated, 1)
                act.wait_ge(u_product, 2 * g + 2)
                f(tanh_g[:], ps_gt[:], ACT.Tanh, bias=half_bg[:], scale=0.5).then_inc(activated, 1)

            act.wait_ge(setup_copied, SETUP_COPIES)
            gate_activations(0, True)
            with act.Fori(1, GROUPS) as g:
                gate_activations(g)

            def stage_states(g):
                if later(g, 1):
                    act.wait_ge(y_product, g)
                f(sloc[:].rearrange("p l h c -> p (l h c)"),
                  local[:, bass.ds((g * SPG + 1) * COLS, GW)], ACT.Copy).then_inc(sloc_ready, 1)

            def normalise_x1(g, b, turn):
                act.wait_ge(norm1_ready, g + 1)
                act.wait_ge(scattered[b], 16 * TOP * TPG * turn)
                if later(g, 2):
                    act.wait_ge(x1b_ready, g - 2)
                for j in range(TPG):
                    ins = f(pay[0][b][:, j, 0:P], z1[:, j, :], ACT.Identity, bias=nb1[:, j:j + 1],
                            scale=rstd1[:, j:j + 1])
                ins.then_inc(x1_ready, 1)

            def copy_x1T(g):
                act.wait_ge(x1_transposed, g + 1)
                if later(g, 1):
                    act.wait_ge(scores_ready, g)
                f(x1T[:], ps_xt[:], ACT.Copy).then_inc(x1T_ready, 1)

            def gap_tanh(g):
                act.wait_ge(gap_ready, g + 1)
                f(m12[:, 5, :], m12[:, 4, :], ACT.Tanh, scale=0.5).then_inc(tanh_ready, 1)

            def copy_weights(g):
                act.wait_ge(wE_transposed, g + 1)
                if later(g, 1):
                    act.wait_ge(bias_product, g)
                f(wET[:], ps_w[0:E, :], ACT.Copy).then_inc(wET_ready, 1)

            def route_group(g, b, turn, last=False):
                if not last:
                    stage_states(g + 1)
                gap_tanh(g)
                if not last:
                    normalise_x1(g + 1, (b + 1) % PAYS, turn)
                    copy_x1T(g + 1)
                copy_weights(g)

            act.wait_ge(state_ready, L)
            stage_states(0)
            normalise_x1(0, 0, 0)
            copy_x1T(0)
            route_group(0, 0, 0)
            with act.Fori(0, (GROUPS - 2) // PAYS) as i:
                for c in range(PAYS):
                    route_group(i * PAYS + 1 + c, (1 + c) % PAYS, i + (2 + c) // PAYS)
            route_group(GROUPS - 1, (GROUPS - 1) % PAYS, None, last=True)

            def copy_xbT(b, q):
                act.wait_ge(xb_transposed, b + 1)
                if later(b, 2):
                    act.wait_ge(up_product, (b - 1) * (BT // 2))
                f(xbT[q % 2][:].rearrange("p s d -> p (s d)"), ps_tx[q % 2][:], ACT.Copy).then_inc(xbT_ready, 1)

            def copy_w1(b, q):
                e = values(act, experts[q % 2], E - 1)
                if later(b, NB):
                    act.wait_ge(up_product, (b - NB + 1) * (BT // 2))
                for s in range(BT):
                    ins = f(w1_now[q][:, s, :], w1_sb[:, bass.ds(e[s] * HID, HID)], ACT.Copy)
                ins.then_inc(w1_copied, 1)

            def gelu(b, q, s, e):
                if s % 2 == 0:
                    act.wait_ge(up_product, b * (BT // 2) + s // 2 + 1)
                if s == 0 and later(b, 2):
                    act.wait_ge(down_product, b - 1)
                for c in range(FC):
                    at = (s % 2) * HID + c * P
                    ins = f(hidden[q % 2][:, s, c, :], ps_hid[(q % 2) * 2 + s // 2][:, at:at + P], ACT.Gelu,
                            bias=bcol[:, bass.ds(e[s] * FC + 2 + c, 1)])
                ins.then_inc(hidden_ready, 1)

            def load_experts(b, q):
                load_batch_of(act, experts[q % 2], tile_expert, b)

            def expert_batch(b, q, turn):
                e = values(act, experts[(q + 1) % 2], E - 1)
                if exists(b + 2):
                    load_experts(b + 2, q + 2)
                for s in range(BT):
                    if exists(b + 1):
                        gelu(b + 1, (q + 1) % NB, s, e)
                    if s == 1 and exists(b + 2):
                        copy_xbT(b + 2, (q + 2) % NB)
                if exists(b + 2):
                    copy_w1(b + 2, (q + 2) % NB)

            experts = [registers(act, f"act_expert{i}_") for i in range(2)]
            act.wait_ge(table_ready, 1)
            for b in range(2):
                load_experts(b, b)
                copy_w1(b, b)
            for b in range(2):
                copy_xbT(b, b)
            e = values(act, experts[0], E - 1)
            for s in range(BT):
                gelu(0, 0, s, e)
            batches(act, expert_batch)

            def weigh_first(g, par):
                act.wait_ge(scale_ready, g + 1)
                if later(g, 2):
                    act.wait_ge(acc0_ready, g - 1)
                for j in range(TPG):
                    ins = f(t0[par][:, j, :],
                            yin[:, bass.ds((g * TPG + j) * TOP, 1), 0:P].rearrange("p a d -> p (a d)"),
                            ACT.Copy, scale=scale[par][:, j, 0:1])
                ins.then_inc(t0_ready, 1)

            def normalise_out(g, par, turn):
                act.wait_ge(norm2_ready, g + 1)
                if turn is not None:
                    act.wait_ge(out_stored[par], 16 * turn)
                for j in range(TPG):
                    ins = f(obuf[par][:, j, :], acc[par][:, j, :], ACT.Identity, bias=nb2[par][:, j:j + 1],
                            scale=rstd2[par][:, j:j + 1])
                ins.then_inc(out_ready, 1)

            weigh_first(0, 0)
            weigh_first(1, 1)
            for g in range(2):
                normalise_out(g, g, None)
                weigh_first(g + 2, g)
            with act.Fori(1, GROUPS // 2 - 1) as i:
                for par in range(2):
                    normalise_out(2 * i + par, par, i)
                    weigh_first(2 * i + par + 2, par)
            for par in range(2):
                normalise_out(GROUPS - 2 + par, par, GROUPS // 2 - 1)

        @block.vector
        def _(dve):
            v = nc.vector
            cp, tt, ts, stt = v.tensor_copy, v.tensor_tensor, v.tensor_scalar, v.scalar_tensor_tensor

            def halves_sum_and_variance(steps, st, tmp, q, n, eps):
                me, mo, qe, qo = st[:, 0:n, 1], st[:, 0:n, 4], st[:, 0:n, 2], st[:, 0:n, 5]
                d, s, dd = (tmp[:, i, 0:n] for i in range(3))
                steps.step(tt(d, me, mo, ALU.subtract))
                steps.step(tt(s, me, mo, ALU.add))
                steps.link(tt(q, qe, qo, ALU.add))
                steps.step(stt(dd, d, 0.25, d, ALU.mult, ALU.mult))
                steps.link(ts(q, q, 1.0 / P, eps, ALU.mult, ALU.add))
                steps.link(tt(q, q, dd, ALU.add))
                return s

            def rsqrt(steps, q, tmp, n):
                a, y = tmp[:, 4, 0:n], tmp[:, 5, 0:n]
                yi = y.bitcast(I32)
                steps.link(ts(yi, q.bitcast(I32), 1, None, ALU.logical_shift_right))
                steps.link(ts(yi, yi, -1.0, float(RSQRT_MAGIC), ALU.mult, ALU.add))
                for _ in range(3):
                    steps.link(tt(a, y, y, ALU.mult))
                    steps.link(stt(a, a, -0.5, q, ALU.mult, ALU.mult))
                    steps.link(stt(y, a, 1.5, y, ALU.add, ALU.mult))
                return y

            dve.wait_ge(setup_transposed, 1)
            cp(wT[:, 0:2, :].rearrange("p k d -> p (k d)"), ps_setup[:, 0:2 * P]).then_inc(setup_copied, 1)
            ts(wT[:, 2, :], ps_setup[:, 2 * P:3 * P], 0.5, None, ALU.mult).then_inc(setup_copied, 1)
            cp(wT[:, 3, :], ps_setup[:, 3 * P:4 * P]).then_inc(setup_copied, 1)
            cp(pq[:, 0, 1, :], ps_small[:, 0:P]).then_inc(setup_copied, 1)
            cp(bcol[:], ps_small[:, P:P + ROWS]).then_inc(setup_copied, 1)
            ts(half_bg[:], ps_small[:, P + 1:P + 2], 0.5, None, ALU.mult).then_inc(setup_copied, 1)

            def copy_xT(g, par, first=False):
                dve.wait_ge(x_transposed, g + 1)
                if not first:
                    dve.wait_ge(u_product, 2 * (g - 1))
                cp(xT[par][:], ps_xt[:]).then_inc(xT_ready, 1)

            def make_u(g, par, first=False):
                dve.wait_ge(activated, 2 * g + 2)
                if not first:
                    dve.wait_ge(state_product, SPG * (g - 1))
                stt(u[par][:], tanh_g[:], 1.0, gelu_u[:], ALU.add, ALU.mult).then_inc(u_ready, 1)

            def copy_state(g, l):
                s = g * SPG + l
                dve.wait_ge(state_product, s + 1)
                cp(local[:, block_of(s + 1)], ps_state[l][:, 0:COLS]).then_inc(state_ready, 1)

            def copy_power(k, par):
                dve.wait_ge(squared, k)
                cp(power[par][:].rearrange("p a d -> p (a d)"), ps_pow[:, 0:2 * P])
                cp(pq[:, bass.ds(k, 1), :, :].rearrange("p k a d -> p (k a d)"), ps_pow[:, 0:2 * P])\
                    .then_inc(power_ready, 1)

            def mixer_group(g, par, first=False):
                copy_state(g, 0)
                copy_power(g + 2, par)
                copy_xT(g + 1, 1 - par, first)
                copy_state(g, 1)
                make_u(g + 1, 1 - par, first)

            copy_xT(0, 0, True)
            copy_power(1, 1)
            make_u(0, 0, True)
            mixer_group(0, 0, True)
            with dve.Fori(0, GROUPS // 2 - 1) as i:
                mixer_group(2 * i + 1, 1)
                mixer_group(2 * i + 2, 0)
            copy_state(GROUPS - 1, 0)
            copy_power(SQUARINGS, 1)
            copy_state(GROUPS - 1, 1)

            dve.wait_ge(zeros_ready, 2)
            dve.wait_ge(state_ready, L)
            cp(ends[:, :, 1:CH + 1], local[:, L * COLS:(L + 1) * COLS].rearrange("p (b c) -> p b c", b=NSEQ))\
                .then_inc(ends_ready, 1)
            for n, (k, src, dst, width) in enumerate(R_CHAIN):
                dve.wait_ge(r_product, n + 1)
                cp(R[:, dst:dst + width, :].rearrange("p l d -> p (l d)"), ps_small[:, 0:width * P]).then_inc(r_ready, 1)
                d = 1 << n
                dve.wait_ge(carry_product, n + 1)
                dve.wait_ge(ends_ready, n + 1)
                tt(ends[:, :, 1 + d:CH + 1], ends[:, :, 1 + d:CH + 1],
                   ps_carry[:, 0:NSEQ * (CH - d)].rearrange("p (b c) -> p b c", b=NSEQ), ALU.add).then_inc(ends_ready, 1)
            dve.wait_ge(ends_ready, CARRY_STEPS + 1)
            cp(carry[:].rearrange("p (b c) -> p b c", b=NSEQ), ends[:, :, 0:CH]).then_inc(carry_ready, 1)

            first = Steps(dve, first_steps, FIRST_STEPS)
            route = Steps(dve, route_steps, ROUTE_STEPS)

            def first_norm(g):
                dve.wait_ge(y_product, g + 1)
                dve.wait_ge(xd_ready, 1)
                if later(g, 1):
                    dve.wait_ge(x1_ready, g)
                    dve.wait_ge(first_steps, g * FIRST_STEPS)
                first.open(g)
                tt(z1[:].rearrange("p (h l) d -> p h l d", h=HALF),
                   ps_y[:].rearrange("p (h l d) -> p h l d", h=HALF, l=SPG),
                   x_all[:, :, bass.ds(g * SPG, SPG), :], ALU.add).then_inc(z1_ready, 1)
                dve.wait_ge(z1_ready, g + 1)
                for j in range(TPG):
                    first.step(v.bn_stats(st1[:, j, :], z1[:, j, :]))
                first.wait()

            def first_norm_scales(g):
                s = halves_sum_and_variance(first, st1, tmp1, tmp1[:, 3, :], TPG, EPS1)
                y = rsqrt(first, tmp1[:, 3, :], tmp1, TPG)
                first.step(cp(rstd1[:], y))
                stt(nb1[:], s, -0.5, y, ALU.mult, ALU.mult).then_inc(norm1_ready, 1)
                dve.wait_ge(norm1_ready, g + 1)

            def second_payload(g, b, turn):
                dve.wait_ge(scattered[b], 16 * TOP * TPG * turn)
                for j in range(TPG):
                    first.step(ts(pay[1][b][:, j, 0:P], z1[:, j, :], rstd1[:, j:j + 1], nb1[:, j:j + 1],
                                  ALU.mult, ALU.add))
                for k in range(TOP):
                    first.step(cp(pay[k][b][:, :, P:XW].bitcast(I32).rearrange("p j a -> p (j a)"),
                                  ids[:, k, bass.ds(g, 1), :].rearrange("p g j -> p (g j)")))
                first.close()

            eq1, oh1, s2, eq2, oh2, both, diff, place, part = (sel[:, i] for i in range(9))
            m1, r1, m2, r2, gap, th = (m12[:, i, :] for i in range(6))

            def spread(a):
                return a.unsqueeze(2).broadcast_to([P, TPG, E])

            def top2(g):
                dve.wait_ge(scores_ready, g + 1)
                route.wait()
                sc = ps_score[:, 0:TPG * E].rearrange("p (j e) -> p j e", e=E)
                route.link(v.tensor_reduce(m1, sc, AX.X, ALU.max))
                route.link(tt(eq1, sc, spread(m1), ALU.is_equal))
                route.link(tt(eq1, eq1, rev[:], ALU.mult))
                route.link(v.tensor_reduce(r1, eq1, AX.X, ALU.max))
                route.link(tt(oh1, eq1, spread(r1), ALU.is_equal))
                route.link(stt(s2, oh1, -3.0e38, sc, ALU.mult, ALU.add))
                route.link(v.tensor_reduce(m2, s2, AX.X, ALU.max))
                tt(gap, m2, m1, ALU.subtract).then_inc(gap_ready, 1)
                route.link(tt(eq2, s2, spread(m2), ALU.is_equal))
                route.link(tt(eq2, eq2, rev[:], ALU.mult))
                route.link(v.tensor_reduce(r2, eq2, AX.X, ALU.max))
                route.link(tt(oh2, eq2, spread(r2), ALU.is_equal))
                route.link(tt(both, oh1, oh2, ALU.add))
                route.step(tt(diff, oh2, oh1, ALU.subtract))
                if later(g, 1):
                    dve.wait_ge(ranks_ready, g)
                route.step(cp(chosen[:], both))
                route.link(cp(seen[:, 0, :], seen[:, TPG, :]))
                for j in range(TPG):
                    ins = tt(seen[:, j + 1, :], seen[:, j, :], both[:, j, :], ALU.add)
                    if j < TPG - 1:
                        route.link(ins)
                    else:
                        ins.then_inc(seen_ready, 1)

            def destinations(g, b):
                dve.wait_ge(ranks_ready, g + 1)
                rk = ps_score[:, RANK0:RANK0 + TPG * E].rearrange("p (j e) -> p j e", e=E)
                route.link(tt(place, rk, bucket0[:], ALU.add))
                for k, oh in enumerate((oh1, oh2)):
                    route.link(tt(part, oh, place, ALU.mult))
                    with nc.allow_low_precision(reason="row numbers, exact in float32, to int32"):
                        ins = v.tensor_reduce(dest[b][:, k, :], part, AX.X, ALU.add)
                    if k == 0:
                        route.link(ins)
                    else:
                        ins.then_inc(dest_ready, 1)

            def weights(g):
                dve.wait_ge(tanh_ready, g + 1)
                if later(g, 1):
                    dve.wait_ge(wE_transposed, g)
                for k in range(TOP):
                    route.step(ts(weight[:, k, bass.ds(g * TPG, TPG)], th, (-0.5, 0.5)[k], 0.5, ALU.mult, ALU.add))
                route.link(tt(diff, diff, spread(th), ALU.mult))
                route.link(tt(both, both, diff, ALU.add))
                ts(wE[:], both, 0.5, None, ALU.mult).then_inc(wE_ready, 1)
                route.close()

            def add_bias(g, b):
                dve.wait_ge(bias_product, g + 1)
                dve.wait_ge(x1_ready, g + 1)
                tt(x1b[:, bass.ds(g * TPG, TPG), :], ps_w[:].rearrange("p (j d) -> p j d", d=P),
                   pay[0][b][:, :, 0:P], ALU.add).then_inc(x1b_ready, 1)

            def route_group(g, b, turn, last=False):
                route.open(g)
                top2(g)
                if not last:
                    first_norm(g + 1)
                destinations(g, b)
                if not last:
                    first_norm_scales(g + 1)
                    second_payload(g + 1, (b + 1) % PAYS, turn)
                weights(g)
                add_bias(g, b)

            first_norm(0)
            first_norm_scales(0)
            second_payload(0, 0, 0)
            route_group(0, 0, 0)
            with dve.Fori(0, (GROUPS - 2) // PAYS) as i:
                for c in range(PAYS):
                    route_group(i * PAYS + 1 + c, (1 + c) % PAYS, i + (2 + c) // PAYS)
            route_group(GROUPS - 1, (GROUPS - 1) % PAYS, None, last=True)

            table = Steps(dve, table_steps, TABLE_STEPS)
            tokens, tiles, upto, skip = (cnt[:, i, :] for i in range(4))
            every = [1, TILES, E]
            dve.wait_ge(counts_ready, 1)
            table.step(cp(tile_no[:], tile_no_i[:]))
            table.link(cp(tokens, ps_score[0:1, COUNT0:COUNT0 + E]))
            table.link(ts(cnt_i[:], tokens, float(P - 1), None, ALU.add))
            table.link(ts(cnt_i[:], cnt_i[:], 7, None, ALU.logical_shift_right))
            table.link(cp(tiles, cnt_i[:]))
            table.link(v.tensor_tensor_scan(upto, skip, tiles, 0.0, ALU.mult, ALU.add))
            table.step(ts(skip, tiles, -float(P), float(CAP), ALU.mult, ALU.add))
            table.link(tt(passed[:], tile_no[:].unsqueeze(2).broadcast_to(every), upto.unsqueeze(1).broadcast_to(every),
                          ALU.is_ge))
            table.link(v.tensor_reduce(tabf[:, 0, :], passed[:], AX.X, ALU.add))
            table.link(tt(passed[:], passed[:], skip.unsqueeze(1).broadcast_to(every), ALU.mult))
            table.link(v.tensor_reduce(tabf[:, 1, :], passed[:], AX.X, ALU.add))
            ts(tile_expert[:], tabf[:, 0, :], float(E - 1), None, ALU.min)
            tt(pad_row[:], tokens, bucket0[0:1, 0, :], ALU.add)
            table.link(stt(tabf[:, 1, :], tile_no[:], float(P), tabf[:, 1, :], ALU.mult, ALU.add))
            ts(tile_row[:], tabf[:, 1, :], float(PAD_TILE), None, ALU.min).then_inc(table_ready, 1)
            table.close()
            dve.wait_ge(table_ready, 1)

            tile = Steps(dve, tile_steps, TILE_STEPS)
            statistics = Turn(dve, "statistics", 2 * BT, TILE_STEPS, table_ready)

            def load_experts(b, q):
                load_batch_of(dve, experts[q % 2], tile_expert, b)

            def expert_rows(b, q, turn):
                buf, y = zt[q % 2], yb[q % 2]
                e = values(dve, experts[q % 2], E - 1)
                tile.open(b)
                dve.wait_ge(down_product, b + 1)
                tt(buf[:], ps_o[q % 2][:].rearrange("p (s d) -> p s d", d=P), xb[q][:, :, 0:P], ALU.add)\
                    .then_inc(z_ready, 1)
                if later(b, NB):
                    dve.wait_ge(yb_stored[q % 2], 16 * BT * ((NB // 2) * (turn - 1) + q // 2 + 1))
                cp(row_ids[q][:], xb[q][:, :, P:XW].bitcast(I32).rearrange("p s a -> p (s a)")).then_inc(ids_kept, 1)
                dve.wait_ge(z_ready, b + 1)
                for s in range(BT):
                    tile.step(tt(buf[:, s, :], buf[:, s, :], b2bc[:, bass.ds(e[s] * P, P)], ALU.add))
                tile.wait()
                if later(b, 2):
                    dve.wait_ge(yb_stored[q % 2], 16 * BT * ((NB // 2) * turn + q // 2))
                for s in range(BT):
                    tile.step(v.bn_stats(stz[:, s, :], buf[:, s, :]))
                statistics.wait(tile_steps)
                statistics.next()
                for s in range(BT):
                    tile.step(v.bn_aggr(y[:, s, P:YW], stz[:, s, :]))
                tile.wait()
                if exists(b + 1):
                    load_experts(b + 1, q + 1)
                for s in range(BT):
                    ins = stt(y[:, s, 0:P], buf[:, s, :], y[:, s, P:P + 1], gbc[:, bass.ds(e[s] * P, P)],
                              ALU.subtract, ALU.mult)
                ins.then_inc(yb_ready, 1)
                tile.close()

            experts = [registers(dve, f"dve_expert{i}_") for i in range(2)]
            load_experts(0, 0)
            batches(dve, expert_rows)

            early = Steps(dve, scale_steps, SCALE_STEPS)
            late = Steps(dve, out_steps, OUT_STEPS)
            GC = TPG * TOP

            def load_variances(g, q):
                return ts(q, yin[:, bass.ds(g * GC, GC), P + 1:P + 2].rearrange("p a b -> p (a b)"),
                          EPS_MOE, None, ALU.add)

            def scales(g, par, y):
                tt(scale[par][:], y.rearrange("p (j k) -> p j k", k=TOP),
                   weight[:, :, bass.ds(g * TPG, TPG)].rearrange("p k j -> p j k"), ALU.mult).then_inc(scale_ready, 1)

            for g in range(2):
                dve.wait_ge(yin_in[g], 16)
                early.step(load_variances(g, var[:, g * GC:(g + 1) * GC]))
            early.wait()
            y = rsqrt(early, var[:], tmp2, 2 * GC)
            early.close()
            for g in range(2):
                scales(g, g, y[:, g * GC:(g + 1) * GC])

            def output_group(g, par, half, last=False):
                late.open(g)
                dve.wait_ge(acc0_ready, g + 1)
                if later(g, 2):
                    dve.wait_ge(out_ready, g - 1)
                dve.wait_ge(scale_ready, g + 1)
                for j in range(TPG):
                    ins = stt(acc[par][:, j, :],
                              yin[:, bass.ds((g * TPG + j) * TOP + 1, 1), 0:P].rearrange("p a d -> p (a d)"),
                              scale[par][:, j, 1:2], acc0[par][:, j, :], ALU.mult, ALU.add)
                    if j < TPG - 1:
                        late.step(ins)
                    else:
                        ins.then_inc(acc_ready, 1)
                dve.wait_ge(acc_ready, g + 1)
                for j in range(TPG):
                    late.step(v.bn_stats(st2[:, j, :], acc[par][:, j, :]))
                if not last:
                    dve.wait_ge(yin_in[par], 16 * (half + 2))
                    load_variances(g + 2, var[:, TPG:TPG + GC])
                late.wait()
                s = halves_sum_and_variance(late, st2, tmp2, var[:, 0:TPG], TPG, EPS1)
                n = TPG if last else TPG + GC
                y = rsqrt(late, var[:, 0:n], tmp2, n)
                late.step(cp(rstd2[par][:], y[:, 0:TPG]))
                stt(nb2[par][:], s, -0.5, y[:, 0:TPG], ALU.mult, ALU.mult).then_inc(norm2_ready, 1)
                if not last:
                    dve.wait_ge(t0_ready, g + 1)
                    scales(g + 2, par, y[:, TPG:n])
                late.close()

            output_group(0, 0, 0)
            output_group(1, 1, 0)
            with dve.Fori(1, GROUPS // 2 - 1) as i:
                output_group(2 * i, 0, i)
                output_group(2 * i + 1, 1, i)
            output_group(GROUPS - 2, 0, None, last=True)
            output_group(GROUPS - 1, 1, None, last=True)

        @block.gpsimd
        def _(pool):
            gp = nc.gpsimd
            gp.memset(ident[:], 0.0).then_inc(ident_zeroed, 1)
            pool.wait_ge(ident_zeroed, 1)
            gp.affine_select(out=ident[:], in_=ident[:], compare_op=ALU.not_equal, fill=1.0, base=0,
                             pattern=[[-1, P]], channel_multiplier=1).then_inc(ident_ready, 1)
            gp.memset(local[:, 0:COLS], 0.0).then_inc(zeros_ready, 1)
            gp.memset(ends[:], 0.0).then_inc(zeros_ready, 1)
            pool.wait_ge(x_all_in, 16)
            pool.wait_ge(mixer_weights_in, 16 * MIXER_LOADS)
            gp.tensor_tensor(x_all.rearrange("p h l d -> p (h l) d"), x_all.rearrange("p h l d -> p (h l) d"),
                             dbc[:].unsqueeze(1).broadcast_to([P, HALF * L, P]), ALU.add).then_inc(xd_ready, 1)
            gp.memset(before[:], 1.0).then_inc(route_consts_ready, 1)
            gp.memset(pad[:], 0.0).then_inc(route_consts_ready, 1)
            for e in range(E):
                gp.memset(rev[:, :, e], float(E - e))
                gp.memset(bucket0[:, :, e], float(e * CAP))
            gp.memset(ones[:], 1.0)
            gp.memset(seen[:], 0.0)
            gp.memset(cnt[:, 3, :], 1.0).then_inc(route_consts_ready, 1)
            gp.iota(tile_no_i[:], pattern=[[1, TILES]], base=0, channel_multiplier=0)\
                .then_inc(route_consts_ready, 1)
            gp.iota(ids[:].rearrange("p k g (h l) -> p k g h l", h=HALF),
                    pattern=[[1, TOP], [SPG * TOP, GROUPS], [P * L * TOP, HALF], [TOP, SPG]], base=0,
                    channel_multiplier=L * TOP).then_inc(route_consts_ready, 1)
            pool.wait_ge(route_consts_ready, 5)
            gp.affine_select(out=before[:], in_=before[:], compare_op=ALU.is_gt, fill=0.0, base=0,
                             pattern=[[1, P]], channel_multiplier=-1).then_inc(route_consts_ready, 1)
            gp.memset(pad[:, P:XW].bitcast(I32), TOKENS * TOP).then_inc(route_consts_ready, 1)

            def scatter_group(g, b):
                routed.wait(x1_ready, dest_ready)
                for k in range(TOP):
                    for j in range(TPG):
                        pool.indirect_dma_start(
                            buckets, bass.IndirectOffsetOnAxis(ap=dest[b][:, k, j:j + 1], axis=0),
                            pay[k][b][:, j, :], None).then_inc(scattered[b], 16)
                routed.next()

            routed = Turn(pool, "routed", 1, 1, xd_ready)
            scatter_group(0, 0)
            with pool.Fori(0, (GROUPS - 2) // PAYS) as i:
                for c in range(PAYS):
                    scatter_group(i * PAYS + 1 + c, (1 + c) % PAYS)
            scatter_group(GROUPS - 1, (GROUPS - 1) % PAYS)

            def scatter_batch(b, q, turn):
                made.wait(yb_ready)
                for s in range(BT):
                    pool.indirect_dma_start(
                        y_rows, bass.IndirectOffsetOnAxis(ap=row_ids[q][:, s:s + 1], axis=0),
                        yb[q % 2][:, s, :], None, bounds_check=TOKENS * TOP - 1, oob_is_err=False)\
                        .then_inc(yb_stored[q % 2], 16)
                made.next()

            made = Turn(pool, "made", 1, 1, table_ready)
            batches(pool, scatter_batch)

            def add_x1(g, par):
                pool.wait_ge(t0_ready, g + 1)
                if later(g, 2):
                    pool.wait_ge(acc_ready, g - 1)
                gp.tensor_tensor(acc0[par][:], t0[par][:], x1b[:, bass.ds(g * TPG, TPG), :], ALU.add)\
                    .then_inc(acc0_ready, 1)

            pool.wait_ge(x1b_ready, GROUPS)
            add_x1(0, 0)
            add_x1(1, 1)
            with pool.Fori(1, GROUPS // 2) as i:
                add_x1(2 * i, 0)
                add_x1(2 * i + 1, 1)


_INS = ['L0_attn_x', 'L0_attn_W_u', 'L0_attn_b_u', 'L0_attn_W_g', 'L0_attn_b_g', 'L0_attn_A', 'L0_attn_Bm',
        'L0_attn_Cm', 'L0_attn_D', 'L0_ffn_gate_w', 'L0_ffn_w1', 'L0_ffn_b1', 'L0_ffn_w2', 'L0_ffn_b2',
        'L0_ffn_ln_g', 'L0_ffn_ln_b']
_OUTS = [((4, 1024, 128), 'float32')]


def kernel(**inputs):
    import numpy as _np
    import concourse.bacc as _bacc
    from concourse import mybir as _mybir
    from concourse.bass_utils import run_bass_kernel_spmd as _run

    nc = _bacc.Bacc("TRN2", target_bir_lowering=False, num_devices=1)
    arrays, args = {}, []
    for name in _INS:
        a = _np.ascontiguousarray(inputs[name])
        arrays[f"in_{name}_dram"] = a
        args.append(nc.dram_tensor(f"in_{name}_dram", a.shape, _mybir.dt.from_np(a.dtype), kind="ExternalInput").ap())
    for i, (shape, dtype) in enumerate(_OUTS):
        dt = _mybir.dt.from_np(_np.dtype(dtype))
        args.append(nc.dram_tensor(f"out_{i}_dram", shape, dt, kind="ExternalOutput").ap())
    mixer_moe_kernel(nc, *args)
    r = _run(nc, [arrays], core_ids=[0])
    got = tuple(r.results[0][f"out_{i}_dram"] for i in range(len(_OUTS)))
    return got[0]
```

```python
from contextlib import ExitStack
from itertools import chain

import concourse.bass as bass
from concourse import mybir

F32 = mybir.dt.float32
BF16 = mybir.dt.bfloat16
I32 = mybir.dt.int32
ALU = mybir.AluOpType
ACT = mybir.ActivationFunctionType
AX = mybir.AxisListType

P = 128
RSQRT_MAGIC = 0x5F3759DF
R_CHAIN = [(0, None, 0, 1), (0, 0, 1, 1), (1, 0, 2, 2), (2, 0, 4, 4), (3, 0, 8, 4), (3, 4, 12, 4)]
CARRY_STEPS = 6
IDLE_PRODUCTS = 3
NORM_STEPS = 17
FIRST_STEPS = 4 + NORM_STEPS + 1 + 4 + 2
ROUTE_STEPS = 22
TILE_STEPS = 8
OUT_STEPS = NORM_STEPS + 1
ROOT_STEPS = 12
TABLE_STEPS = 12


class Turn:

    def __init__(self, engine, name, first, step, reached):
        self.engine, self.step, self.reached = engine, step, reached
        self.value = engine.alloc_register(name)
        engine.reg_mov(self.value, first)

    def next(self):
        self.engine.reg_add(self.value, self.value, self.step)

    def wait(self, *sems):
        self.engine.wait_ge(self.reached, 1)
        for s in sems:
            self.engine.wait_ge(s, self.value)


class Counted:

    def __init__(self, engine, sem, per_group):
        self.engine, self.sem, self.per_group = engine, sem, per_group
        self.g, self.k = 0, 0

    def open(self, g):
        self.g, self.k = g, 0

    def step(self, instruction):
        instruction.then_inc(self.sem, 1)
        self.k += 1

    def wait(self):
        self.engine.wait_ge(self.sem, self.g * self.per_group + self.k)

    def link(self, instruction):
        self.step(instruction)
        self.wait()

    def close(self):
        assert self.k == self.per_group, self.k


class Steps:

    def __init__(self, engine, sems):
        self.engine, self.sems = engine, sems
        self.g, self.k = 0, 0

    def open(self, g):
        self.g, self.k = g, 0

    def step(self, instruction):
        instruction.then_inc(self.sems[self.k], 1)
        self.k += 1

    def wait(self, before=0):
        if self.k > 0:
            self.engine.wait_ge(self.sems[self.k - 1 - before], self.g + 1)
        else:
            self.wait_last()

    def wait_last(self):
        if later(self.g, 1):
            self.engine.wait_ge(self.sems[-1], self.g)

    def link(self, instruction):
        self.step(instruction)
        self.wait()

    def close(self):
        assert self.k == len(self.sems), self.k


def alone(steps):
    for _ in steps:
        pass


def later(k, n):
    return not isinstance(k, int) or k >= n


def mixer_moe_kernel(nc, x, W_u, b_u, W_g, b_g, A, Bm, Cm, D, gate_w, w1, b1, w2, b2, ln_g, ln_b, out):
    NSEQ, T, DIM = x.shape
    E = gate_w.shape[1]
    HID = w1.shape[2]
    FC = HID // P
    L = 16
    CH = T // L
    HALF = NSEQ * T // (P * L)
    COLS = HALF * P
    SPG = 2
    TPG = SPG * HALF
    GW = TPG * P
    GROUPS = L // SPG
    ROWS = 2 + E * FC
    SQUARINGS = 9
    TOP = 2
    TOKENS = NSEQ * T
    EPS1 = 1e-5
    EPS_MOE = 1e-6
    PAYS = 3
    CAP = TOKENS + P
    PAD_TILE = E * CAP
    XW = DIM + 1
    YW = DIM + 2
    TILES = TOP * TOKENS // P + E
    BT = 4
    ROUNDS = GROUPS // 2
    OT = 2 * TPG
    NB = 4
    PARTS = 3
    BATCHES = TILES // BT
    LOOPED = BATCHES // NB
    assert DIM == P and HALF == 2 and GW == 512 and CH * 2 == P and E == 8 and FC == 2
    assert TILES % BT == 0 and TILES >= TOP * TOKENS // P + E - 1

    xv = x.rearrange("b t d -> (b t) d").rearrange("(h p l) d -> p h l d", h=HALF, p=P)
    ov = out.rearrange("b t d -> (b t) d").rearrange("(h p l) d -> p h l d", h=HALF, p=P)
    buckets = nc.dram_tensor("buckets", (E * CAP + P, XW), F32, kind="Internal").ap()
    y_rows = nc.dram_tensor("y_rows", (TOKENS * TOP, YW), F32, kind="Internal").ap()
    yv = y_rows.rearrange("(h p l k) c -> p h l k c", h=HALF, p=P, k=TOP)

    with ExitStack() as ctx:
        def sb(name, shape, dt=F32):
            return ctx.enter_context(nc.sbuf_tensor(name, shape, dt))

        def sem(name):
            return ctx.enter_context(nc.semaphore(name))

        bank = [ctx.enter_context(nc.psum_tensor(f"bank{i}", [P, 512], F32)) for i in range(8)]
        ps_u, ps_gt, ps_setup, ps_small = bank[0], bank[1], bank[2], bank[3]
        ps_state, ps_pow, ps_xt = [bank[4], bank[5]], bank[6], bank[7]
        ps_carry = bank[2]
        ps_y, ps_score, ps_w = bank[6], bank[0], bank[1]
        ps_tx, ps_hid, ps_o = [bank[4], bank[5]], [bank[6], bank[7], bank[0], bank[1]], [bank[2], bank[3]]
        ps_rank = bank[4]
        COUNT0 = TPG * E

        ident = sb("ident", [P, P])
        before = sb("before", [P, P], BF16)
        ones = sb("ones", [P, P], BF16)
        rev = sb("rev", [P, TPG, E])
        bucket0 = sb("bucket0", [P, TPG, E])
        ids = sb("ids", [P, TOP, GROUPS, TPG], I32)
        tile_no_i = sb("tile_no_i", [1, TILES], I32)
        tile_no = sb("tile_no", [1, TILES])
        pad = sb("pad", [P, XW])
        wraw = sb("wraw", [P, 4, P])
        rows = sb("rows", [ROWS, P])
        bcol = sb("bcol", [P, ROWS])
        table_in = sb("table_in", [P, 1])
        half_bg = sb("half_bg", [P, 1])
        wT = sb("wT", [P, 4, P])
        power = [sb(f"power{i}", [P, 2, P]) for i in range(2)]
        pq = sb("pq", [P, SQUARINGS + 1, 2, P])
        R = sb("R", [P, L, P])
        dbc = sb("dbc", [P, P])
        gate_sb = sb("gate_sb", [P, E])
        w1_sb = sb("w1_sb", [P, E * HID])
        w2_sb = sb("w2_sb", [P, E * FC * P])
        b2_rest = sb("b2_rest", [PARTS, E * P])
        b2_parts = sb("b2_parts", [PARTS, E * P], BF16)
        minus_part = sb("minus_part", [PARTS, PARTS - 1])
        gbc = sb("gbc", [P, E * P])
        lnb_sb = sb("lnb_sb", [TPG * E, TPG, P])
        xin = [sb(f"xin{i}", [P, HALF, SPG, P]) for i in range(2)]
        xT = [sb(f"xT{i}", [P, GW]) for i in range(2)]
        gelu_u = sb("gelu_u", [P, GW])
        tanh_g = sb("tanh_g", [P, GW])
        u = [sb(f"u{i}", [P, GW]) for i in range(2)]
        STATES = (L + 1) * COLS
        YIN = GROUPS * TPG * TOP * YW
        by_token = sb("by_token", [P, max(STATES + HALF * L * P, YIN)])
        local = by_token[:, 0:STATES]
        x_all = by_token[:, STATES:STATES + HALF * L * P].rearrange("p (h l d) -> p h l d", h=HALF, l=L)
        yin = by_token[:, 0:YIN].rearrange("p (a c) -> p a c", c=YW)
        ends = sb("ends", [P, NSEQ, CH + 1])
        carry = sb("carry", [P, COLS])
        sloc = sb("sloc", [P, SPG, HALF, P])
        z1 = sb("z1", [P, TPG, P])
        st1 = sb("st1", [P, TPG, 6])
        tmp1 = sb("tmp1", [P, 6, TPG])
        rstd1 = sb("rstd1", [P, TPG])
        nb1 = sb("nb1", [P, TPG])
        pay = [[sb(f"pay{k}_{i}", [P, TPG, XW]) for i in range(PAYS)] for k in range(TOP)]
        dest = [sb(f"dest{i}", [P, TOP, TPG], I32) for i in range(PAYS)]
        x1T = sb("x1T", [P, GW])
        m12 = sb("m12", [P, 6, TPG])
        sel = sb("sel", [P, 9, TPG, E])
        chosen = sb("chosen", [P, TPG, E], BF16)
        seen = sb("seen", [P, E], BF16)
        counted = sb("counted", [P, E], BF16)
        weight = sb("weight", [P, TOP, GROUPS * TPG])
        wE = sb("wE", [P, TPG, E])
        wET = sb("wET", [TPG * E, P])
        x1b = sb("x1b", [P, GROUPS * TPG, P])
        cnt = sb("cnt", [1, 4, E])
        cnt_i = sb("cnt_i", [1, E], I32)
        passed = sb("passed", [1, TILES, E])
        tabf = sb("tabf", [1, 2, TILES])
        tile_row = sb("tile_row", [1, TILES], I32)
        tile_expert = sb("tile_expert", [1, TILES], I32)
        pad_row = sb("pad_row", [1, E], I32)
        xb = [sb(f"xb{i}", [P, BT, XW]) for i in range(NB)]
        w1_now = [sb(f"w1_now{i}", [P, BT, HID]) for i in range(NB)]
        xbT = [sb(f"xbT{i}", [P, BT, P]) for i in range(2)]
        hidden = [sb(f"hidden{i}", [P, BT, FC, P]) for i in range(2)]
        zt = [sb(f"zt{i}", [P, BT, P]) for i in range(2)]
        stz = sb("stz", [P, BT, 6])
        yb = [sb(f"yb{i}", [P, BT, YW]) for i in range(NB)]
        tmpz = sb("tmpz", [P, 6, BT])
        row_ids = [sb(f"row_ids{i}", [P, BT], I32) for i in range(NB)]
        tmp2 = sb("tmp2", [P, 6, OT])
        scale = sb("scale", [P, GROUPS * TPG, TOP])
        st2 = sb("st2", [P, OT, 6])
        rstd2 = sb("rstd2", [P, GROUPS * TPG])
        nb2 = sb("nb2", [P, GROUPS * TPG])

        mixer_weights_in = sem("mixer_weights_in")
        moe_weights_in = sem("moe_weights_in")
        x_all_in = sem("x_all_in")
        x_in = [sem(f"x_in{i}") for i in range(2)]
        ident_zeroed = sem("ident_zeroed")
        ident_ready = sem("ident_ready")
        zeros_ready = sem("zeros_ready")
        lnb_zeroed = sem("lnb_zeroed")
        route_consts_ready = sem("route_consts_ready")
        setup_transposed = sem("setup_transposed")
        setup_copied = sem("setup_copied")
        squared = sem("squared")
        power_ready = sem("power_ready")
        r_product = sem("r_product")
        r_ready = sem("r_ready")
        x_transposed = sem("x_transposed")
        xT_ready = sem("xT_ready")
        u_product = sem("u_product")
        activated = sem("activated")
        u_ready = sem("u_ready")
        state_product = sem("state_product")
        state_ready = sem("state_ready")
        ends_ready = sem("ends_ready")
        carry_product = sem("carry_product")
        carry_ready = sem("carry_ready")
        xd_ready = sem("xd_ready")
        sloc_ready = sem("sloc_ready")
        y_product = sem("y_product")
        z1_ready = sem("z1_ready")
        first_steps = [sem(f"first_step{k}") for k in range(FIRST_STEPS)]
        route_steps = [sem(f"route_step{k}") for k in range(ROUTE_STEPS)]
        norm1_ready = sem("norm1_ready")
        x1_ready = sem("x1_ready")
        x1_transposed = sem("x1_transposed")
        x1T_ready = sem("x1T_ready")
        scores_ready = sem("scores_ready")
        gap_ready = sem("gap_ready")
        chosen_ready = sem("chosen_ready")
        ranks_ready = sem("ranks_ready")
        dest_ready = sem("dest_ready")
        tanh_ready = sem("tanh_ready")
        wE_ready = sem("wE_ready")
        wE_transposed = sem("wE_transposed")
        wET_ready = sem("wET_ready")
        bias_product = sem("bias_product")
        x1b_ready = sem("x1b_ready")
        groups_left = sem("groups_left")
        scattered = [sem(f"scattered{i}") for i in range(PAYS)]
        counts_ready = sem("counts_ready")
        table_steps = sem("table_steps")
        table_ready = sem("table_ready")
        pad_rows_ready = sem("pad_rows_ready")
        pads_in = sem("pads_in")
        xb_in = [sem(f"xb_in{i}") for i in range(NB)]
        w1_copied = sem("w1_copied")
        xb_transposed = sem("xb_transposed")
        xbT_ready = sem("xbT_ready")
        up_product = sem("up_product")
        hidden_ready = sem("hidden_ready")
        down_product = sem("down_product")
        z_ready = sem("z_ready")
        ids_kept = sem("ids_kept")
        tile_steps = [sem(f"tile_step{k}") for k in range(TILE_STEPS)]
        yb_ready = sem("yb_ready")
        yb_stored = [sem(f"yb_stored{i}") for i in range(NB)]
        yin_in = [sem(f"yin_in{i}") for i in range(ROUNDS)]
        b2_steps = sem("b2_steps")
        root_steps = [sem(f"root_step{k}") for k in range(ROOT_STEPS)]
        out_steps = sem("out_steps")
        scale_ready = sem("scale_ready")
        t0_ready = sem("t0_ready")
        t1_ready = sem("t1_ready")
        sums_ready = sem("sums_ready")
        stats2_ready = sem("stats2_ready")
        norm2_ready = sem("norm2_ready")
        out_ready = sem("out_ready")
        last_out_ready = sem("last_out_ready")
        out_stored = sem("out_stored")

        block = ctx.enter_context(nc.Block())

        MIXER_LOADS = 9
        MOE_LOADS = 5 + TPG
        SETUP_COPIES = 6

        def block_of(l):
            return bass.ds(l * COLS, COLS)

        def registers(engine, name):
            return [engine.alloc_register(f"{name}{s}") for s in range(BT)]

        def load_batch_of(engine, regs, table, b):
            engine.load(regs, table[0:1, bass.ds(b * BT, BT)])

        def values(engine, regs, top):
            return [engine.snap(r, min_val=0, max_val=top) for r in regs]

        def batches(engine, one):
            for b in range(NB):
                one(b, b, 0)
            with engine.Fori(1, LOOPED) as i:
                for q in range(NB):
                    one(i * NB + q, q, i)
            for b in range(LOOPED * NB, BATCHES):
                one(b, b % NB, b // NB)

        def exists(b):
            return not isinstance(b, int) or b < BATCHES

        def scatters_done(engine):
            for i in range(PAYS):
                engine.wait_ge(scattered[i], 16 * TOP * TPG * len(range(i, GROUPS, PAYS)))

        @block.sync
        def _(sp):
            def load_group(g, half, par, reused):
                if reused:
                    sp.wait_ge(x_transposed, g - 1)
                sp.dma_start(xin[par][:], xv[:, :, bass.ds(g * SPG, SPG), :]).then_inc(x_in[par], 16)

            load_group(0, 0, 0, False)
            for k, w in enumerate((W_u, W_g, Bm, Cm)):
                sp.dma_start(wraw[:, k, :], w).then_inc(mixer_weights_in, 16)
            sp.dma_start(pq[:, 0, 0, :], A).then_inc(mixer_weights_in, 16)
            sp.dma_start(rows[0:1, :], b_u.rearrange("(a n) -> a n", a=1)).then_inc(mixer_weights_in, 16)
            sp.dma_start(rows[1:2, :], b_g.rearrange("(a n) -> a n", a=1)).then_inc(mixer_weights_in, 16)
            sp.dma_start(rows[2:ROWS, :], b1.rearrange("e (f p) -> (e f) p", p=P)).then_inc(mixer_weights_in, 16)
            sp.dma_start(dbc[:], D.partition_broadcast(P)).then_inc(mixer_weights_in, 16)
            load_group(1, 0, 1, False)
            sp.dma_start(x_all, xv).then_inc(x_all_in, 16)
            with sp.Fori(1, GROUPS // 2) as i:
                load_group(2 * i, i, 0, True)
                load_group(2 * i + 1, i, 1, True)
            sp.dma_start(gate_sb[:], gate_w).then_inc(moe_weights_in, 16)
            sp.wait_ge(lnb_zeroed, 1)
            for j in range(TPG):
                sp.dma_start(lnb_sb[j * E:(j + 1) * E, j, :], ln_b).then_inc(moe_weights_in, 16)
            sp.dma_start(w1_sb[:].rearrange("p (e f) -> p e f", e=E), w1.rearrange("e d f -> d e f"))\
                .then_inc(moe_weights_in, 16)
            sp.dma_start(w2_sb[:].rearrange("p (e c d) -> p e c d", e=E, c=FC),
                         w2.rearrange("e (c f) d -> f e c d", c=FC)).then_inc(moe_weights_in, 16)
            sp.dma_start(b2_rest[:], b2.rearrange("e d -> (e d)").partition_broadcast(PARTS)).then_inc(moe_weights_in, 16)
            sp.dma_start(gbc[:], ln_g.rearrange("e d -> (e d)").partition_broadcast(P)).then_inc(moe_weights_in, 16)

            sp.wait_ge(route_consts_ready, 7)
            sp.dma_start(buckets[PAD_TILE:PAD_TILE + P, :], pad[:]).then_inc(pads_in, 16)
            sp.wait_ge(pad_rows_ready, 1)
            ends_of = registers(sp, "bucket_end")
            for e0 in range(0, E, BT):
                sp.load(ends_of, pad_row[0:1, e0:e0 + BT])
                for r in values(sp, ends_of, E * CAP - P):
                    sp.dma_start(buckets[bass.ds(r, P), :], pad[:]).then_inc(pads_in, 16)
            sp.wait_ge(table_ready, 1)
            sp.wait_ge(pads_in, 16 * (E + 1))
            scatters_done(sp)

            def load_batch(b, q, turn):
                load_batch_of(sp, first_rows, tile_row, b)
                rows_at = values(sp, first_rows, PAD_TILE)
                if later(b, NB):
                    sp.wait_ge(ids_kept, b - NB + 1)
                for s, r in enumerate(rows_at):
                    sp.dma_start(xb[q][:, s, :], buckets[bass.ds(r, P), :]).then_inc(xb_in[q], 16)

            first_rows = registers(sp, "first_row")
            batches(sp, load_batch)

            for q in range(NB):
                sp.wait_ge(yb_stored[q], 16 * BT * len(range(q, BATCHES, NB)))

            for g in range(GROUPS):
                c = TPG * TOP
                sp.dma_start(yin[:, g * c:(g + 1) * c, :].rearrange("p (h l k) c -> p h l k c", h=HALF, k=TOP),
                             yv[:, :, g * SPG:(g + 1) * SPG, :, :]).then_inc(yin_in[g // 2], 16)

            def store_out(g):
                sp.dma_start(ov[:, :, bass.ds(g * SPG, SPG), :],
                             x1b[:, bass.ds(g * TPG, TPG), :].rearrange("p (h l) d -> p h l d", h=HALF))\
                    .then_inc(out_stored, 16)

            with sp.Fori(0, GROUPS - 2) as g:
                sp.wait_ge(out_ready, g + 1)
                store_out(g)
            sp.wait_ge(last_out_ready, 1)
            store_out(GROUPS - 1)
            sp.wait_ge(out_ready, GROUPS - 1)
            store_out(GROUPS - 2)
            sp.wait_ge(out_stored, 16 * GROUPS)

        @block.tensor
        def _(pe):
            mm, tr = nc.tensor.matmul, nc.tensor.transpose

            def transpose_x(g, half, par, first=False):
                pe.wait_ge(x_in[par], 16 * (half + 1))
                if not first:
                    pe.wait_ge(xT_ready, g)
                for l in range(SPG):
                    for h in range(HALF):
                        c = (l * HALF + h) * P
                        ins = tr(ps_xt[:, c:c + P], xin[par][:, h, l, :], ident[:])
                ins.then_inc(x_transposed, 1)

            def gates(g, par, first=False):
                pe.wait_ge(xT_ready, g + 1)
                if not first:
                    pe.wait_ge(activated, 2 * g)
                mm(ps_u[:], wT[:, 0, :], xT[par][:], start=True, stop=True).then_inc(u_product, 1)
                mm(ps_gt[:], wT[:, 1, :], xT[par][:], start=True, stop=True).then_inc(u_product, 1)

            def state_step(g, l, par, first=False):
                s = g * SPG + l
                pe.wait_ge(u_ready, g + 1)
                if not first:
                    pe.wait_ge(state_ready, s - 1)
                mm(ps_state[l][:, 0:COLS], wT[:, 2, :], u[par][:, l * COLS:(l + 1) * COLS], start=True, stop=False)
                pe.wait_ge(state_ready, s)
                mm(ps_state[l][:, 0:COLS], pq[:, 0, 1, :], local[:, block_of(s)], start=False, stop=True)\
                    .then_inc(state_product, 1)

            def square(k, a, at):
                if k is not None:
                    pe.wait_ge(power_ready, k)
                mm(ps_pow[:, 0:P], at, a, start=True, stop=True)
                mm(ps_pow[:, P:2 * P], a, at, start=True, stop=True).then_inc(squared, 1)

            def rows_of_R(n):
                k, src, dst, width = R_CHAIN[n]
                pe.wait_ge(r_ready, n)
                rhs = wT[:, 3, :] if src is None else R[:, src:src + width, :].rearrange("p l d -> p (l d)")
                mm(ps_small[:, 0:width * P], pq[:, k, 0, :], rhs, start=True, stop=True).then_inc(r_product, 1)

            def mixer_group(g, half, par, first=False):
                state_step(g, 0, par, first)
                transpose_x(g + 2, half + 1, par)
                square(g + 1, power[1 - par][:, 0, :], power[1 - par][:, 1, :])
                state_step(g, 1, par, first)
                gates(g + 2, par)

            def last_mixer_group(g, par):
                for l in range(SPG):
                    state_step(g, l, par)
                    if g == GROUPS - 2:
                        rows_of_R(l)
                square(g + 1, power[1 - par][:, 0, :], power[1 - par][:, 1, :])

            pe.wait_ge(ident_ready, 1)
            transpose_x(0, 0, 0, True)
            pe.wait_ge(mixer_weights_in, 16 * MIXER_LOADS)
            for k in range(4):
                tr(ps_setup[:, k * P:(k + 1) * P], wraw[:, k, :], ident[:])
            tr(ps_small[:, 0:P], pq[:, 0, 0, :], ident[:])
            mm(ps_small[:, P:P + ROWS], rows[:], ident[0:ROWS, 0:ROWS], start=True, stop=True)\
                .then_inc(setup_transposed, 1)
            pe.wait_ge(setup_copied, SETUP_COPIES)
            gates(0, 0, True)
            transpose_x(1, 0, 1)
            gates(1, 1)
            square(None, pq[:, 0, 0, :], pq[:, 0, 1, :])
            pe.wait_ge(zeros_ready, 1)
            mixer_group(0, 0, 0, True)
            mixer_group(1, 0, 1)
            with pe.Fori(1, GROUPS // 2 - 1) as i:
                mixer_group(2 * i, i, 0)
                mixer_group(2 * i + 1, i, 1)
            pe.wait_ge(power_ready, 3)
            for par in range(2):
                last_mixer_group(GROUPS - 2 + par, par)

            for n in range(CARRY_STEPS):
                d = 1 << n
                pe.wait_ge(power_ready, 4 + n)
                pe.wait_ge(ends_ready, n + 1)
                mm(ps_carry[:, 0:NSEQ * (CH - d)].rearrange("p (b c) -> p b c", b=NSEQ),
                   pq[:, 4 + n, 1, :], ends[:, :, 1:CH + 1 - d], start=True, stop=True).then_inc(carry_product, 1)
                if SPG + n < len(R_CHAIN):
                    rows_of_R(SPG + n)

            def mixer_out(g):
                pe.wait_ge(sloc_ready, g + 1)
                if later(g, 1):
                    pe.wait_ge(z1_ready, g)
                for h in range(HALF):
                    for l in range(SPG):
                        c = (h * SPG + l) * P
                        mm(ps_y[:, c:c + P], sloc[:, l, h, :], wT[:, 3, :], start=True, stop=False)
                        ins = mm(ps_y[:, c:c + P], carry[:, h * P:(h + 1) * P],
                                 R[:, bass.ds(g * SPG + l, 1), :].rearrange("p l d -> p (l d)"),
                                 start=False, stop=True)
                ins.then_inc(y_product, 1)

            def transpose_x1(g, b):
                pe.wait_ge(x1_ready, g + 1)
                if later(g, 1):
                    pe.wait_ge(x1T_ready, g)
                for j in range(TPG):
                    ins = tr(ps_xt[:, j * P:(j + 1) * P], pay[0][b][:, j, 0:P], ident[:])
                ins.then_inc(x1_transposed, 1)

            def scores(g):
                pe.wait_ge(x1T_ready, g + 1)
                for j in range(TPG):
                    ins = mm(ps_score[:, j * E:(j + 1) * E], x1T[:, j * P:(j + 1) * P], gate_sb[:],
                             start=True, stop=True)
                ins.then_inc(scores_ready, 1)

            def ranks(g):
                pe.wait_ge(chosen_ready, g + 1)
                o = ps_rank[:, 0:TPG * E]
                mm(o, before[:], chosen[:].rearrange("p j e -> p (j e)"), start=True, stop=False)
                for j in range(TPG - 1):
                    n = TPG - 1 - j
                    mm(ps_rank[:, (j + 1) * E:TPG * E].rearrange("p (j e) -> p j e", e=E), ones[:],
                       chosen[:, j:j + 1, :].broadcast_to([P, n, E]), start=False, stop=False)
                mm(o.rearrange("p (j e) -> p j e", e=E), ones[:], seen[:].unsqueeze(1).broadcast_to([P, TPG, E]),
                   start=False, stop=True).then_inc(ranks_ready, 1)

            def transpose_weights(g):
                pe.wait_ge(wE_ready, g + 1)
                if later(g, 1):
                    pe.wait_ge(x1b_ready, g)
                tr(ps_w[0:TPG * E, 0:P], wE[:].rearrange("p j e -> p (j e)"), ident[:]).then_inc(wE_transposed, 1)

            def bias(g):
                pe.wait_ge(wET_ready, g + 1)
                mm(ps_w[:], wET[:], lnb_sb[:].rearrange("k j d -> k (j d)"), start=True, stop=True)\
                    .then_inc(bias_product, 1)

            def route_group(g, b, last=False):
                if not last:
                    mixer_out(g + 1)
                if later(g, 1):
                    ranks(g - 1)
                transpose_x1(g, b)
                scores(g)
                if later(g, 1):
                    transpose_weights(g - 1)
                    bias(g - 1)

            pe.wait_ge(carry_ready, 1)
            pe.wait_ge(r_ready, len(R_CHAIN))
            pe.wait_ge(route_consts_ready, 7)
            pe.wait_ge(moe_weights_in, 16 * MOE_LOADS)
            mixer_out(0)
            route_group(0, 0)
            with pe.Fori(0, (GROUPS - 2) // PAYS) as i:
                for c in range(PAYS):
                    route_group(i * PAYS + 1 + c, (1 + c) % PAYS)
            route_group(GROUPS - 1, (GROUPS - 1) % PAYS, last=True)
            ranks(GROUPS - 1)
            pe.wait_ge(dest_ready, GROUPS)
            mm(ps_rank[:, COUNT0:COUNT0 + E], ones[:], seen[:], start=True, stop=True).then_inc(counts_ready, 1)
            transpose_weights(GROUPS - 1)
            bias(GROUPS - 1)

            def transpose_batch(b, q, turn):
                pe.wait_ge(xb_in[q], 16 * BT * (turn + 1))
                if later(b, 2):
                    pe.wait_ge(xbT_ready, b - 1)
                for s in range(BT):
                    ins = tr(ps_tx[q % 2][:, s * P:(s + 1) * P], xb[q][:, s, 0:P], ident[:])
                ins.then_inc(xb_transposed, 1)

            def up(b, q, h):
                if h == 0:
                    pe.wait_ge(xbT_ready, b + 1)
                    pe.wait_ge(w1_copied, (b + 1) * (BT // 2))
                if later(b, 2):
                    pe.wait_ge(hidden_ready, (b - 2) * BT + 2 * h + 2)
                for s in range(2 * h, 2 * h + 2):
                    for c in range(FC):
                        at = (s % 2) * HID + c * P
                        ins = mm(ps_hid[(q % 2) * 2 + h][:, at:at + P], w1_now[q][:, s, c * P:(c + 1) * P],
                                 xbT[q % 2][:, s, :], start=True, stop=True)
                ins.then_inc(up_product, 1)

            def down(b, q, s, e):
                pe.wait_ge(hidden_ready, b * BT + s + 1)
                if s == 0 and later(b, 2):
                    pe.wait_ge(z_ready, b - 1)
                for c in range(FC):
                    mm(ps_o[q % 2][:, s * P:(s + 1) * P], hidden[q % 2][:, s, c, :],
                             w2_sb[:, bass.ds(e * (FC * P) + c * P, P)], start=(c == 0), stop=False)
                ins = mm(ps_o[q % 2][:, s * P:(s + 1) * P], ones[0:PARTS, :], b2_parts[:, bass.ds(e * P, P)],
                         start=False, stop=True)
                if s == BT - 1:
                    ins.then_inc(down_product, 1)

            def expert_batch(b, q, turn):
                load_batch_of(pe, experts, tile_expert, b)
                e = values(pe, experts, E - 1)
                for h in range(BT // 2):
                    if exists(b + 1):
                        up(b + 1, (q + 1) % NB, h)
                    if h == 1 and exists(b + 2):
                        transpose_batch(b + 2, (q + 2) % NB, turn + (q + 2) // NB)
                    for s in range(2 * h, 2 * h + 2):
                        down(b, q, s, e[s])

            experts = registers(pe, "pe_expert")
            pe.wait_ge(table_ready, 1)
            pe.wait_ge(x1b_ready, GROUPS)
            scatters_done(pe)
            pe.wait_ge(b2_steps, 2 * PARTS - 1)
            for _ in range(IDLE_PRODUCTS):
                mm(ps_hid[0][:], ident[:], R[:, 0:TPG, :].rearrange("p l d -> p (l d)"), start=True, stop=True)
            transpose_batch(0, 0, 0)
            transpose_batch(1, 1, 0)
            for h in range(BT // 2):
                up(0, 0, h)
            batches(pe, expert_batch)

        @block.scalar
        def _(act):
            f = nc.scalar.activation

            def gate_activations(g, first=False):
                act.wait_ge(u_product, 2 * g + 1)
                if not first:
                    act.wait_ge(u_ready, g)
                f(gelu_u[:], ps_u[:], ACT.Gelu, bias=bcol[:, 0:1]).then_inc(activated, 1)
                act.wait_ge(u_product, 2 * g + 2)
                f(tanh_g[:], ps_gt[:], ACT.Tanh, bias=half_bg[:], scale=0.5).then_inc(activated, 1)

            act.wait_ge(ident_ready, 1)
            f(table_in[:], ident[:, 0:1], ACT.Gelu)
            act.wait_ge(setup_copied, SETUP_COPIES)
            gate_activations(0, True)
            with act.Fori(1, GROUPS) as g:
                gate_activations(g)

            def stage_states(g):
                if later(g, 1):
                    act.wait_ge(y_product, g)
                f(sloc[:].rearrange("p l h c -> p (l h c)"),
                  local[:, bass.ds((g * SPG + 1) * COLS, GW)], ACT.Copy).then_inc(sloc_ready, 1)

            def normalise_x1(g, b):
                act.wait_ge(norm1_ready, g + 1)
                if later(g, 2):
                    act.wait_ge(groups_left, g - 1)
                for j in range(TPG):
                    ins = f(pay[0][b][:, j, 0:P], z1[:, j, :], ACT.Identity, bias=nb1[:, j:j + 1],
                            scale=rstd1[:, j:j + 1])
                ins.then_inc(x1_ready, 1)

            def copy_x1T(g):
                act.wait_ge(x1_transposed, g + 1)
                if later(g, 1):
                    act.wait_ge(scores_ready, g)
                f(x1T[:], ps_xt[:], ACT.Copy).then_inc(x1T_ready, 1)

            def gap_tanh(g):
                act.wait_ge(gap_ready, g + 1)
                f(m12[:, 5, :], m12[:, 4, :], ACT.Tanh, scale=0.5).then_inc(tanh_ready, 1)

            def copy_weights(g):
                act.wait_ge(wE_transposed, g + 1)
                if later(g, 1):
                    act.wait_ge(bias_product, g)
                f(wET[:], ps_w[0:TPG * E, 0:P], ACT.Copy).then_inc(wET_ready, 1)

            def route_group(g, b, last=False):
                if not last:
                    stage_states(g + 1)
                if later(g, 1):
                    gap_tanh(g - 1)
                normalise_x1(g, b)
                copy_x1T(g)
                if later(g, 1):
                    copy_weights(g - 1)

            for n, (_, _, dst, width) in enumerate(R_CHAIN):
                act.wait_ge(r_product, n + 1)
                f(R[:, dst:dst + width, :].rearrange("p l d -> p (l d)"), ps_small[:, 0:width * P], ACT.Copy)\
                    .then_inc(r_ready, 1)

            act.wait_ge(state_ready, L)
            stage_states(0)
            route_group(0, 0)
            with act.Fori(0, (GROUPS - 2) // PAYS) as i:
                for c in range(PAYS):
                    route_group(i * PAYS + 1 + c, (1 + c) % PAYS)
            route_group(GROUPS - 1, (GROUPS - 1) % PAYS, last=True)
            gap_tanh(GROUPS - 1)
            copy_weights(GROUPS - 1)

            def copy_xbT(b, q):
                act.wait_ge(xb_transposed, b + 1)
                if later(b, 2):
                    act.wait_ge(up_product, (b - 1) * (BT // 2))
                f(xbT[q % 2][:].rearrange("p s d -> p (s d)"), ps_tx[q % 2][:], ACT.Copy).then_inc(xbT_ready, 1)

            def copy_w1(b, q, h):
                e = values(act, experts[q % 2], E - 1)
                if h == 0 and later(b, NB):
                    act.wait_ge(up_product, (b - NB + 1) * (BT // 2))
                for s in range(2 * h, 2 * h + 2):
                    ins = f(w1_now[q][:, s, :], w1_sb[:, bass.ds(e[s] * HID, HID)], ACT.Copy)
                ins.then_inc(w1_copied, 1)

            def gelu(b, q, s, e):
                if s % 2 == 0:
                    act.wait_ge(up_product, b * (BT // 2) + s // 2 + 1)
                if s == 0 and later(b, 2):
                    act.wait_ge(down_product, b - 1)
                for c in range(FC):
                    at = (s % 2) * HID + c * P
                    ins = f(hidden[q % 2][:, s, c, :], ps_hid[(q % 2) * 2 + s // 2][:, at:at + P], ACT.Gelu,
                            bias=bcol[:, bass.ds(e[s] * FC + 2 + c, 1)])
                ins.then_inc(hidden_ready, 1)

            def load_experts(b, q):
                load_batch_of(act, experts[q % 2], tile_expert, b)

            def expert_batch(b, q, turn):
                e = values(act, experts[(q + 1) % 2], E - 1)
                if exists(b + 2):
                    load_experts(b + 2, q + 2)
                for h in range(BT // 2):
                    if exists(b + 2):
                        copy_w1(b + 2, (q + 2) % NB, h)
                    if h == 1 and exists(b + 2):
                        copy_xbT(b + 2, (q + 2) % NB)
                    if exists(b + 1):
                        for s in range(2 * h, 2 * h + 2):
                            gelu(b + 1, (q + 1) % NB, s, e)

            experts = [registers(act, f"act_expert{i}_") for i in range(2)]
            act.wait_ge(table_ready, 1)
            for b in range(2):
                load_experts(b, b)
                for h in range(BT // 2):
                    copy_w1(b, b, h)
            copy_xbT(0, 0)
            copy_xbT(1, 1)
            e = values(act, experts[0], E - 1)
            for s in range(BT):
                gelu(0, 0, s, e)
            batches(act, expert_batch)

            def weigh_first(r):
                act.wait_ge(scale_ready, r + 1)
                for j in range(OT):
                    row = yin[:, bass.ds((r * OT + j) * TOP, 1), 0:P].rearrange("p a d -> p (a d)")
                    ins = f(row, row, ACT.Copy, scale=scale[:, bass.ds(r * OT + j, 1), 0:1].rearrange("p a k -> p (a k)"))
                    if j % TPG == TPG - 1:
                        ins.then_inc(t0_ready, 1)

            def normalise_out(r, tiles=OT):
                act.wait_ge(norm2_ready, r + 1)
                for j in range(tiles):
                    t = r * OT + j
                    ins = f(x1b[:, bass.ds(t, 1), :].rearrange("p a d -> p (a d)"),
                            yin[:, bass.ds(t * TOP + 1, 1), 0:P].rearrange("p a d -> p (a d)"), ACT.Identity,
                            bias=nb2[:, bass.ds(t, 1)], scale=rstd2[:, bass.ds(t, 1)])
                    if j % TPG == TPG - 1:
                        ins.then_inc(out_ready, 1)

            weigh_first(0)
            weigh_first(1)
            with act.Fori(0, ROUNDS - 2) as r:
                weigh_first(r + 2)
                normalise_out(r)
            normalise_out(ROUNDS - 2)
            normalise_out(ROUNDS - 1, TPG)

        @block.vector
        def _(dve):
            v = nc.vector
            cp, tt, ts, stt = v.tensor_copy, v.tensor_tensor, v.tensor_scalar, v.scalar_tensor_tensor

            def variance(steps, st, tmp, q, n, eps):
                me, mo, qe, qo = st[:, 0:n, 1], st[:, 0:n, 4], st[:, 0:n, 2], st[:, 0:n, 5]
                d, dd = tmp[:, 0, 0:n], tmp[:, 2, 0:n]
                steps.wait()
                steps.step(tt(d, me, mo, ALU.subtract))
                steps.step(tt(half_sums(tmp, n), me, mo, ALU.add))
                steps.step(tt(q, qe, qo, ALU.add))
                yield
                steps.wait()
                steps.step(stt(dd, d, 0.25, d, ALU.mult, ALU.mult))
                steps.step(ts(q, q, 1.0 / P, eps, ALU.mult, ALU.add))
                yield
                steps.wait()
                steps.step(tt(q, q, dd, ALU.add))
                yield

            def half_sums(tmp, n):
                return tmp[:, 1, 0:n]

            def root(tmp, n):
                return tmp[:, 5, 0:n]

            def rsqrt(steps, q, tmp, n):
                a, y = tmp[:, 4, 0:n], root(tmp, n)
                yi = y.bitcast(I32)
                steps.wait()
                steps.step(ts(yi, q.bitcast(I32), 1, None, ALU.logical_shift_right))
                yield
                steps.wait()
                steps.step(ts(yi, yi, -1.0, float(RSQRT_MAGIC), ALU.mult, ALU.add))
                yield
                for _ in range(3):
                    steps.wait()
                    steps.step(tt(a, y, y, ALU.mult))
                    yield
                    steps.wait()
                    steps.step(stt(a, a, -0.5, q, ALU.mult, ALU.mult))
                    yield
                    steps.wait()
                    steps.step(stt(y, a, 1.5, y, ALU.add, ALU.mult))
                    yield

            def copy_xT(g, par, first=False):
                dve.wait_ge(x_transposed, g + 1)
                if not first:
                    dve.wait_ge(u_product, 2 * (g - 1))
                cp(xT[par][:], ps_xt[:]).then_inc(xT_ready, 1)

            def make_u(g, par, first=False):
                dve.wait_ge(activated, 2 * g + 2)
                if not first:
                    dve.wait_ge(state_product, SPG * (g - 1))
                stt(u[par][:], tanh_g[:], 1.0, gelu_u[:], ALU.add, ALU.mult).then_inc(u_ready, 1)

            def copy_state(g, l):
                s = g * SPG + l
                dve.wait_ge(state_product, s + 1)
                cp(local[:, block_of(s + 1)], ps_state[l][:, 0:COLS]).then_inc(state_ready, 1)

            def copy_power(k, par):
                dve.wait_ge(squared, k)
                cp(power[par][:].rearrange("p a d -> p (a d)"), ps_pow[:, 0:2 * P])
                cp(pq[:, bass.ds(k, 1), :, :].rearrange("p k a d -> p (k a d)"), ps_pow[:, 0:2 * P])\
                    .then_inc(power_ready, 1)

            def mixer_group(g, par):
                copy_state(g, 0)
                copy_xT(g + 2, par)
                copy_state(g, 1)
                copy_power(g + 2, par)
                make_u(g + 2, par)

            copy_xT(0, 0, True)
            dve.wait_ge(setup_transposed, 1)
            cp(wT[:, 0:2, :].rearrange("p k d -> p (k d)"), ps_setup[:, 0:2 * P]).then_inc(setup_copied, 1)
            ts(wT[:, 2, :], ps_setup[:, 2 * P:3 * P], 0.5, None, ALU.mult).then_inc(setup_copied, 1)
            cp(wT[:, 3, :], ps_setup[:, 3 * P:4 * P]).then_inc(setup_copied, 1)
            cp(pq[:, 0, 1, :], ps_small[:, 0:P]).then_inc(setup_copied, 1)
            cp(bcol[:], ps_small[:, P:P + ROWS]).then_inc(setup_copied, 1)
            ts(half_bg[:], ps_small[:, P + 1:P + 2], 0.5, None, ALU.mult).then_inc(setup_copied, 1)
            copy_xT(1, 1, True)
            make_u(0, 0, True)
            copy_power(1, 1)
            make_u(1, 1, True)
            mixer_group(0, 0)
            mixer_group(1, 1)
            with dve.Fori(1, GROUPS // 2 - 1) as i:
                mixer_group(2 * i, 0)
                mixer_group(2 * i + 1, 1)
            for l in range(SPG):
                copy_state(GROUPS - 2, l)
            copy_power(GROUPS, 0)
            for l in range(SPG):
                copy_state(GROUPS - 1, l)
            dve.wait_ge(zeros_ready, 2)
            dve.wait_ge(state_ready, L)
            cp(ends[:, :, 1:CH + 1], local[:, L * COLS:(L + 1) * COLS].rearrange("p (b c) -> p b c", b=NSEQ))\
                .then_inc(ends_ready, 1)
            copy_power(GROUPS + 1, 1)
            for n in range(CARRY_STEPS):
                d = 1 << n
                dve.wait_ge(carry_product, n + 1)
                dve.wait_ge(ends_ready, n + 1)
                tt(ends[:, :, 1 + d:CH + 1], ends[:, :, 1 + d:CH + 1],
                   ps_carry[:, 0:NSEQ * (CH - d)].rearrange("p (b c) -> p b c", b=NSEQ), ALU.add).then_inc(ends_ready, 1)
            dve.wait_ge(ends_ready, CARRY_STEPS + 1)
            cp(carry[:].rearrange("p (b c) -> p b c", b=NSEQ), ends[:, :, 0:CH]).then_inc(carry_ready, 1)

            first = Steps(dve, first_steps)
            route = Steps(dve, route_steps)

            def make_z1(g):
                dve.wait_ge(y_product, g + 1)
                dve.wait_ge(xd_ready, 1)
                if later(g, 1):
                    dve.wait_ge(x1_ready, g)
                    dve.wait_ge(first_steps[-1], g)
                first.open(g)
                tt(z1[:].rearrange("p (h l) d -> p h l d", h=HALF),
                   ps_y[:].rearrange("p (h l d) -> p h l d", h=HALF, l=SPG),
                   x_all[:, :, bass.ds(g * SPG, SPG), :], ALU.add).then_inc(z1_ready, 1)

            def first_statistics(g):
                dve.wait_ge(z1_ready, g + 1)
                for j in range(TPG):
                    first.step(v.bn_stats(st1[:, j, :], z1[:, j, :]))

            def first_norm_scales(g):
                yield from variance(first, st1, tmp1, tmp1[:, 3, :], TPG, EPS1)
                yield from rsqrt(first, tmp1[:, 3, :], tmp1, TPG)
                first.wait()
                first.step(cp(rstd1[:], root(tmp1, TPG)))
                stt(nb1[:], half_sums(tmp1, TPG), -0.5, root(tmp1, TPG), ALU.mult, ALU.mult).then_inc(norm1_ready, 1)

            def second_payload(g, b):
                if later(g, 2):
                    dve.wait_ge(groups_left, g - 1)
                dve.wait_ge(norm1_ready, g + 1)
                for j in range(TPG):
                    first.step(ts(pay[1][b][:, j, 0:P], z1[:, j, :], rstd1[:, j:j + 1], nb1[:, j:j + 1],
                                  ALU.mult, ALU.add))
                for k in range(TOP):
                    first.step(cp(pay[k][b][:, :, P:XW].bitcast(I32).rearrange("p j a -> p (j a)"),
                                  ids[:, k, bass.ds(g, 1), :].rearrange("p g j -> p (g j)")))
                first.close()

            eq1, oh1, s2, eq2, oh2, diff, place, part0, part1 = (sel[:, i] for i in range(9))
            parts = (part0, part1)
            m1, r1, m2, r2, gap, th = (m12[:, i, :] for i in range(6))

            def spread(a):
                return a.unsqueeze(2).broadcast_to([P, TPG, E])

            def top2(g):
                dve.wait_ge(scores_ready, g + 1)
                sc = ps_score[:, 0:TPG * E].rearrange("p (j e) -> p j e", e=E)
                route.wait()
                route.step(v.tensor_reduce(m1, sc, AX.X, ALU.max))
                yield
                route.wait()
                route.step(tt(eq1, sc, spread(m1), ALU.is_equal))
                yield
                route.wait()
                route.step(tt(eq1, eq1, rev[:], ALU.mult))
                yield
                route.wait()
                route.step(v.tensor_reduce(r1, eq1, AX.X, ALU.max))
                yield
                route.wait()
                route.step(tt(oh1, eq1, spread(r1), ALU.is_equal))
                yield
                route.wait()
                route.step(stt(s2, oh1, -3.0e38, sc, ALU.mult, ALU.add))
                yield
                route.wait()
                route.step(v.tensor_reduce(m2, s2, AX.X, ALU.max))
                yield
                route.wait()
                tt(gap, m2, m1, ALU.subtract).then_inc(gap_ready, 1)
                route.step(tt(eq2, s2, spread(m2), ALU.is_equal))
                yield
                route.wait()
                route.step(tt(eq2, eq2, rev[:], ALU.mult))
                yield
                route.wait()
                route.step(v.tensor_reduce(r2, eq2, AX.X, ALU.max))
                yield
                route.wait()
                route.step(tt(oh2, eq2, spread(r2), ALU.is_equal))
                yield
                if later(g, 1):
                    dve.wait_ge(ranks_ready, g)
                route.wait()
                tt(chosen[:], oh1, oh2, ALU.add).then_inc(chosen_ready, 1)

            def count_choices(g):
                route.step(tt(diff, oh2, oh1, ALU.subtract))
                yield
                dve.wait_ge(chosen_ready, g + 1)
                with nc.allow_low_precision(reason="counts up to 4 are exact in bfloat16"):
                    route.step(v.tensor_reduce(counted[:], chosen[:].rearrange("p j e -> p e j"), AX.X, ALU.add))
                yield

            def destinations_and_weights(g, b):
                dve.wait_ge(ranks_ready, g + 1)
                route.wait()
                rk = ps_rank[:, 0:TPG * E].rearrange("p (j e) -> p j e", e=E)
                route.step(tt(place, rk, bucket0[:], ALU.add))
                route.step(tt(seen[:], seen[:], counted[:], ALU.add))
                route.wait()
                for k, oh in enumerate((oh1, oh2)):
                    route.step(tt(parts[k], oh, place, ALU.mult))
                dve.wait_ge(tanh_ready, g + 1)
                route.step(tt(diff, diff, spread(th), ALU.mult))
                route.wait(1)
                with nc.allow_low_precision(reason="row numbers, exact in float32, to int32"):
                    route.step(v.tensor_reduce(dest[b][:, 0, :], parts[0], AX.X, ALU.add))
                    v.tensor_reduce(dest[b][:, 1, :], parts[1], AX.X, ALU.add).then_inc(dest_ready, 1)
                for k in range(TOP):
                    route.step(ts(weight[:, k, bass.ds(g * TPG, TPG)], th, (-0.5, 0.5)[k], 0.5, ALU.mult, ALU.add))
                route.wait(3)
                route.step(tt(diff, diff, chosen[:], ALU.add))
                route.close()

            def finish_weights(g):
                dve.wait_ge(route_steps[-1], g + 1)
                if later(g, 1):
                    dve.wait_ge(wE_transposed, g)
                ts(wE[:], diff, 0.5, None, ALU.mult).then_inc(wE_ready, 1)

            def add_bias(g, b):
                dve.wait_ge(bias_product, g + 1)
                tt(x1b[:, bass.ds(g * TPG, TPG), :], ps_w[:].rearrange("p (j d) -> p j d", d=P),
                   pay[0][b][:, :, 0:P], ALU.add).then_inc(x1b_ready, 1)

            def route_group(g, b, last=False):
                if not last:
                    make_z1(g + 1)
                if later(g, 1):
                    finish_weights(g - 1)
                if not last:
                    first_statistics(g + 1)
                route.open(g)
                choice, scales = top2(g), iter(()) if last else first_norm_scales(g + 1)
                for _ in choice:
                    next(scales, None)
                counts = count_choices(g)
                for _ in scales:
                    next(counts, None)
                alone(counts)
                if later(g, 1):
                    add_bias(g - 1, (b - 1) % PAYS)
                if not last:
                    second_payload(g + 1, (b + 1) % PAYS)
                destinations_and_weights(g, b)

            make_z1(0)
            first_statistics(0)
            alone(first_norm_scales(0))
            second_payload(0, 0)
            route_group(0, 0)
            with dve.Fori(0, (GROUPS - 2) // PAYS) as i:
                for c in range(PAYS):
                    route_group(i * PAYS + 1 + c, (1 + c) % PAYS)
            route_group(GROUPS - 1, (GROUPS - 1) % PAYS, last=True)
            finish_weights(GROUPS - 1)
            table = Counted(dve, table_steps, TABLE_STEPS)
            tokens, tiles, upto, skip = (cnt[:, i, :] for i in range(4))
            every = [1, TILES, E]
            table.step(cp(tile_no[:], tile_no_i[:]))
            dve.wait_ge(counts_ready, 1)
            table.link(cp(tokens, ps_rank[0:1, COUNT0:COUNT0 + E]))
            tt(pad_row[:], tokens, bucket0[0:1, 0, :], ALU.add).then_inc(pad_rows_ready, 1)
            table.link(ts(cnt_i[:], tokens, float(P - 1), None, ALU.add))
            table.link(ts(cnt_i[:], cnt_i[:], 7, None, ALU.logical_shift_right))
            table.link(cp(tiles, cnt_i[:]))
            table.step(v.tensor_tensor_scan(upto, skip, tiles, 0.0, ALU.mult, ALU.add))
            table.wait()
            table.step(ts(skip, tiles, -float(P), float(CAP), ALU.mult, ALU.add))
            table.link(tt(passed[:], tile_no[:].unsqueeze(2).broadcast_to(every), upto.unsqueeze(1).broadcast_to(every),
                          ALU.is_ge))
            table.link(v.tensor_reduce(tabf[:, 0, :], passed[:], AX.X, ALU.add))
            table.link(tt(passed[:], passed[:], skip.unsqueeze(1).broadcast_to(every), ALU.mult))
            table.link(v.tensor_reduce(tabf[:, 1, :], passed[:], AX.X, ALU.add))
            ts(tile_expert[:], tabf[:, 0, :], float(E - 1), None, ALU.min)
            table.link(stt(tabf[:, 1, :], tile_no[:], float(P), tabf[:, 1, :], ALU.mult, ALU.add))
            ts(tile_row[:], tabf[:, 1, :], float(PAD_TILE), None, ALU.min).then_inc(table_ready, 1)
            table.close()
            dve.wait_ge(table_ready, 1)
            add_bias(GROUPS - 1, (GROUPS - 1) % PAYS)

            dve.wait_ge(moe_weights_in, 16 * MOE_LOADS)
            split = Counted(dve, b2_steps, 2 * PARTS - 1)
            split.link(cp(b2_parts[:], b2_rest[:]))
            for k in range(PARTS - 1):
                split.link(stt(b2_rest[:], b2_parts[:], minus_part[:, k:k + 1], b2_rest[:], ALU.mult, ALU.add))
                split.link(cp(b2_parts[:], b2_rest[:]))
            split.close()

            tile = Steps(dve, tile_steps)
            statistics = Turn(dve, "statistics", 1, 1, table_ready)

            def load_experts(b, q):
                load_batch_of(dve, experts[q % 2], tile_expert, b)

            roots = Steps(dve, root_steps)

            def finish_rows(b, q):
                roots.open(b)
                variances = yb[q][:, :, P + 1:YW].rearrange("p s a -> p (s a)")
                roots.wait()
                roots.step(ts(tmpz[:, 3, :], variances, EPS_MOE, None, ALU.add))
                yield
                yield from rsqrt(roots, tmpz[:, 3, :], tmpz, BT)
                roots.wait()
                cp(variances, root(tmpz, BT)).then_inc(yb_ready, 1)
                roots.close()

            def expert_rows(b, q, turn):
                buf, y = zt[q % 2], yb[q]
                e = values(dve, experts[q % 2], E - 1)
                before_it = finish_rows(b - 1, (q - 1) % NB) if later(b, 1) else iter(())
                tile.open(b)
                dve.wait_ge(down_product, b + 1)
                tt(buf[:], ps_o[q % 2][:].rearrange("p (s d) -> p s d", d=P), xb[q][:, :, 0:P], ALU.add)\
                    .then_inc(z_ready, 1)
                if later(b, NB):
                    dve.wait_ge(yb_stored[q], 16 * BT * turn)
                cp(row_ids[q][:], xb[q][:, :, P:XW].bitcast(I32).rearrange("p s a -> p (s a)")).then_inc(ids_kept, 1)
                next(before_it, None)
                dve.wait_ge(z_ready, b + 1)
                for s in range(BT):
                    tile.step(v.bn_stats(stz[:, s, :], buf[:, s, :]))
                    next(before_it, None)
                statistics.wait(tile_steps[BT - 1])
                statistics.next()
                for s in range(BT):
                    tile.step(v.bn_aggr(y[:, s, P:YW], stz[:, s, :]))
                    next(before_it, None)
                tile.wait()
                for s in range(BT):
                    stt(y[:, s, 0:P], buf[:, s, :], y[:, s, P:P + 1], gbc[:, bass.ds(e[s] * P, P)],
                        ALU.subtract, ALU.mult)
                    next(before_it, None)
                alone(before_it)
                if exists(b + 1):
                    load_experts(b + 1, q + 1)
                tile.close()

            experts = [registers(dve, f"dve_expert{i}_") for i in range(2)]
            load_experts(0, 0)
            batches(dve, expert_rows)
            alone(finish_rows(BATCHES - 1, (BATCHES - 1) % NB))

            late = Counted(dve, out_steps, OUT_STEPS)

            def scales(r):
                dve.wait_ge(yin_in[r], 32)
                tt(scale[:, bass.ds(r * OT, OT), :],
                   yin[:, bass.ds(r * OT * TOP, OT * TOP), P + 1:YW].rearrange("p (j k) a -> p j (k a)", k=TOP),
                   weight[:, :, bass.ds(r * OT, OT)].rearrange("p k j -> p j k"), ALU.mult).then_inc(scale_ready, 1)

            def weigh_second(r):
                dve.wait_ge(scale_ready, r + 1)
                for j in range(OT):
                    t = r * OT + j
                    row = yin[:, bass.ds(t * TOP + 1, 1), 0:P].rearrange("p a d -> p (a d)")
                    ins = stt(row, row, scale[:, bass.ds(t, 1), 1:2].rearrange("p a k -> p (a k)"),
                              x1b[:, bass.ds(t, 1), :].rearrange("p a d -> p (a d)"), ALU.mult, ALU.add)
                    if j % TPG == TPG - 1:
                        ins.then_inc(t1_ready, 1)
                    yield

            def second_statistics(r):
                if later(r, 1):
                    dve.wait_ge(out_steps, (r - 1) * OUT_STEPS + 3)
                for j in range(OT):
                    if j % TPG == 0:
                        dve.wait_ge(sums_ready, r * (OT // TPG) + j // TPG + 1)
                    ins = v.bn_stats(st2[:, j, :], yin[:, bass.ds((r * OT + j) * TOP + 1, 1), 0:P]
                                     .rearrange("p a d -> p (a d)"))
                    if j == OT - 1:
                        ins.then_inc(stats2_ready, 1)
                    yield

            def second_norm_scales(r):
                late.open(r)
                dve.wait_ge(stats2_ready, r + 1)
                if later(r, 1):
                    dve.wait_ge(norm2_ready, r)
                yield from variance(late, st2, tmp2, tmp2[:, 3, :], OT, EPS1)
                yield from rsqrt(late, tmp2[:, 3, :], tmp2, OT)
                late.wait()
                late.step(cp(rstd2[:, bass.ds(r * OT, OT)], root(tmp2, OT)))
                stt(nb2[:, bass.ds(r * OT, OT)], half_sums(tmp2, OT), -0.5, root(tmp2, OT), ALU.mult, ALU.mult)\
                    .then_inc(norm2_ready, 1)
                late.close()

            scales(0)
            alone(weigh_second(0))
            scales(1)
            alone(weigh_second(1))
            alone(second_statistics(0))
            for r in range(ROUNDS):
                beside = []
                if r + 2 < ROUNDS:
                    scales(r + 2)
                    beside.append(weigh_second(r + 2))
                if r + 1 < ROUNDS:
                    beside.append(second_statistics(r + 1))
                beside = chain(*beside)
                for _ in second_norm_scales(r):
                    next(beside, None)
                alone(beside)
            dve.wait_ge(norm2_ready, ROUNDS)
            for t in range((GROUPS - 1) * TPG, GROUPS * TPG):
                ins = ts(x1b[:, t, :], yin[:, t * TOP + 1, 0:P], rstd2[:, t:t + 1], nb2[:, t:t + 1], ALU.mult, ALU.add)
            ins.then_inc(last_out_ready, 1)

        @block.gpsimd
        def _(pool):
            gp = nc.gpsimd
            gp.memset(ident[:], 0.0).then_inc(ident_zeroed, 1)
            pool.wait_ge(ident_zeroed, 1)
            gp.affine_select(out=ident[:], in_=ident[:], compare_op=ALU.not_equal, fill=1.0, base=0,
                             pattern=[[-1, P]], channel_multiplier=1).then_inc(ident_ready, 1)
            gp.memset(local[:, 0:COLS], 0.0).then_inc(zeros_ready, 1)
            gp.memset(ends[:], 0.0).then_inc(zeros_ready, 1)
            pool.wait_ge(x_all_in, 16)
            pool.wait_ge(mixer_weights_in, 16 * MIXER_LOADS)
            gp.tensor_tensor(x_all.rearrange("p h l d -> p (h l) d"), x_all.rearrange("p h l d -> p (h l) d"),
                             dbc[:].unsqueeze(1).broadcast_to([P, HALF * L, P]), ALU.add).then_inc(xd_ready, 1)
            gp.memset(lnb_sb[:], 0.0).then_inc(lnb_zeroed, 1)
            gp.memset(before[:], 1.0).then_inc(route_consts_ready, 1)
            gp.memset(pad[:], 0.0).then_inc(route_consts_ready, 1)
            for e in range(E):
                gp.memset(rev[:, :, e], float(E - e))
                gp.memset(bucket0[:, :, e], float(e * CAP))
            gp.memset(ones[:], 1.0)
            gp.memset(minus_part[:], -1.0)
            gp.memset(seen[:], 0.0)
            gp.memset(cnt[:, 3, :], 1.0).then_inc(route_consts_ready, 1)
            gp.iota(tile_no_i[:], pattern=[[1, TILES]], base=0, channel_multiplier=0)\
                .then_inc(route_consts_ready, 1)
            gp.iota(ids[:].rearrange("p k g (h l) -> p k g h l", h=HALF),
                    pattern=[[1, TOP], [SPG * TOP, GROUPS], [P * L * TOP, HALF], [TOP, SPG]], base=0,
                    channel_multiplier=L * TOP).then_inc(route_consts_ready, 1)
            pool.wait_ge(route_consts_ready, 5)
            for k in range(PARTS - 1):
                gp.memset(minus_part[0:k + 1, k:k + 1], 0.0)
            gp.affine_select(out=before[:], in_=before[:], compare_op=ALU.is_gt, fill=0.0, base=0,
                             pattern=[[1, P]], channel_multiplier=-1).then_inc(route_consts_ready, 1)
            gp.memset(pad[:, P:XW].bitcast(I32), TOKENS * TOP).then_inc(route_consts_ready, 1)

            def scatter_group(g, b, turn):
                routed.wait(x1_ready, dest_ready)
                for k in range(TOP):
                    if k == 1:
                        if later(g, 1):
                            pool.wait_ge(scattered[(b - 1) % PAYS], 16 * TOP * TPG * turn)
                        pool.sem_inc(groups_left, 1)
                    for j in range(TPG):
                        pool.indirect_dma_start(
                            buckets, bass.IndirectOffsetOnAxis(ap=dest[b][:, k, j:j + 1], axis=0),
                            pay[k][b][:, j, :], None).then_inc(scattered[b], 16)
                routed.next()

            routed = Turn(pool, "routed", 1, 1, xd_ready)
            scatter_group(0, 0, None)
            with pool.Fori(0, (GROUPS - 2) // PAYS) as i:
                for c in range(PAYS):
                    scatter_group(i * PAYS + 1 + c, (1 + c) % PAYS, i + 1)
            scatter_group(GROUPS - 1, (GROUPS - 1) % PAYS, (GROUPS - 2) // PAYS + 1)

            def scatter_batch(b, q, turn):
                made.wait(yb_ready)
                for s in range(BT):
                    pool.indirect_dma_start(
                        y_rows, bass.IndirectOffsetOnAxis(ap=row_ids[q][:, s:s + 1], axis=0),
                        yb[q][:, s, :], None, bounds_check=TOKENS * TOP - 1, oob_is_err=False)\
                        .then_inc(yb_stored[q], 16)
                made.next()

            made = Turn(pool, "made", 1, 1, table_ready)
            batches(pool, scatter_batch)

            with pool.Fori(0, GROUPS) as g:
                pool.wait_ge(t0_ready, g + 1)
                pool.wait_ge(t1_ready, g + 1)
                first_rows, second_rows = (yin[:, bass.ds(g * TPG * TOP, TPG * TOP), 0:P]
                                           .rearrange("p (j k) d -> p j k d", k=TOP)[:, :, k, :] for k in range(TOP))
                gp.tensor_tensor(second_rows, second_rows, first_rows, ALU.add).then_inc(sums_ready, 1)


_INS = ['L0_attn_x', 'L0_attn_W_u', 'L0_attn_b_u', 'L0_attn_W_g', 'L0_attn_b_g', 'L0_attn_A', 'L0_attn_Bm',
        'L0_attn_Cm', 'L0_attn_D', 'L0_ffn_gate_w', 'L0_ffn_w1', 'L0_ffn_b1', 'L0_ffn_w2', 'L0_ffn_b2',
        'L0_ffn_ln_g', 'L0_ffn_ln_b']
_OUTS = [((4, 1024, 128), 'float32')]


def kernel(**inputs):
    import numpy as _np
    import concourse.bacc as _bacc
    from concourse import mybir as _mybir
    from concourse.bass_utils import run_bass_kernel_spmd as _run

    nc = _bacc.Bacc("TRN2", target_bir_lowering=False, num_devices=1)
    arrays, args = {}, []
    for name in _INS:
        a = _np.ascontiguousarray(inputs[name])
        arrays[f"in_{name}_dram"] = a
        args.append(nc.dram_tensor(f"in_{name}_dram", a.shape, _mybir.dt.from_np(a.dtype), kind="ExternalInput").ap())
    for i, (shape, dtype) in enumerate(_OUTS):
        dt = _mybir.dt.from_np(_np.dtype(dtype))
        args.append(nc.dram_tensor(f"out_{i}_dram", shape, dt, kind="ExternalOutput").ap())
    mixer_moe_kernel(nc, *args)
    r = _run(nc, [arrays], core_ids=[0])
    got = tuple(r.results[0][f"out_{i}_dram"] for i in range(len(_OUTS)))
    return got[0]
```
